# Optimizing a Trainium2 kernel written in Bass

```python
import numpy as np
import jax
import jax.numpy as jnp

def _softmax(x, axis=-1):
    return jax.nn.softmax(x, axis=axis)

def _gelu(x):
    return jax.nn.gelu(x, approximate=True)

def _silu(x):
    return jax.nn.silu(x)

def _sigmoid(x):
    return jax.nn.sigmoid(x)

def _layernorm(x, axis=-1, eps=1e-05):
    m = jnp.mean(x, axis=axis, keepdims=True)
    v = jnp.var(x, axis=axis, keepdims=True)
    return (x - m) / jnp.sqrt(v + eps)

def _scatter_add(tgt, idx, src, axis=0):
    return tgt.at[idx].add(src)

def _segment_sum(src, seg, n):
    return jax.ops.segment_sum(src, seg, n)
kernel_name = 'mk_adaln_d1_jaxref_r8_43be52'

def setup_inputs(seed: int=0):
    np.random.seed(seed)
    _w = jnp.asarray

    def _L0_attn_setup():
        import jax, jax.numpy as jnp
        import numpy as np
        DIM = 128
        HEADS = 16
        HEAD_DIM = 64
        key = jax.random.key(seed)
        ks = jax.random.split(key, 6)
        inner = HEADS * HEAD_DIM
        s = 0.02
        return {'x': jax.random.normal(ks[0], (2, 256, DIM), dtype=jnp.float32), 'Wq': jax.random.normal(ks[1], (DIM, inner), dtype=jnp.float32) * s, 'Wk': jax.random.normal(ks[2], (DIM, inner), dtype=jnp.float32) * s, 'Wv': jax.random.normal(ks[3], (DIM, inner), dtype=jnp.float32) * s, 'Wo': jax.random.normal(ks[4], (inner, DIM), dtype=jnp.float32) * s, 'bo': jax.random.normal(ks[5], (DIM,), dtype=jnp.float32) * s}
    _L0_attn_in = _L0_attn_setup()

    def _L0_ffn_setup():
        import jax, jax.numpy as jnp
        import numpy as np
        DIM = 128
        DEPTH = 6
        HEADS = 16
        DIM_HEAD = 64
        WINDOW = 32
        INNER = HEADS * DIM_HEAD
        DIM_INNER = int(DIM * 4 * 2 / 3)
        QK_SCALE = 8.0

        def shift_tokens(t):
            a, s = jnp.split(t, 2, -1)
            s = jnp.pad(s, ((0, 0), (1, 0), (0, 0)))[:, :-1]
            return jnp.concatenate([a, s], -1)

        def l2norm(t):
            return t / jnp.maximum(jnp.linalg.norm(t, axis=-1, keepdims=True), 1e-12)

        def rotate_half(x):
            x1, x2 = jnp.split(x, 2, -1)
            return jnp.concatenate([-x2, x1], -1)

        def rotary_tables(n):
            half = jnp.arange(0, DIM_HEAD, 2, dtype=jnp.float32)
            inv_freq = 1.0 / 10000.0 ** (half / DIM_HEAD)
            t = jnp.arange(n, dtype=jnp.float32)
            freqs = t[:, None] * inv_freq[None, :]
            freqs = jnp.concatenate([freqs, freqs], -1)
            base_scale = (half + 0.4 * DIM_HEAD) / (1.4 * DIM_HEAD)
            power = (t - n // 2) / (WINDOW // 2)
            scale = base_scale[None, :] ** power[:, None]
            scale = jnp.concatenate([scale, scale], -1)
            return (freqs, scale)

        def local_attention(q, k, v):
            b, h, n, d = q.shape
            w = WINDOW
            nw = n // w
            bq = q.reshape(b, h, nw, w, d)
            bk = k.reshape(b, h, nw, w, d)
            bv = v.reshape(b, h, nw, w, d)

            def look(t):
                p = jnp.pad(t, ((0, 0), (0, 0), (1, 0), (0, 0), (0, 0)))
                return jnp.concatenate([p[:, :, :nw], p[:, :, 1:]], axis=3)
            bk2, bv2 = (look(bk), look(bv))
            seq = jnp.arange(n).reshape(nw, w)
            seq_p = jnp.pad(seq, ((1, 0), (0, 0)), constant_values=-1)
            jt = jnp.concatenate([seq_p[:nw], seq_p[1:]], axis=1)
            it = seq[:, :, None]
            jb = jt[:, None, :]
            mask = (it < jb) | (it > jb + w) | (jb == -1)
            sim = jnp.einsum('bhwie,bhwje->bhwij', bq, bk2) * QK_SCALE
            sim = jnp.where(mask, -jnp.finfo(sim.dtype).max, sim)
            attn = jax.nn.softmax(sim, -1)
            out = jnp.einsum('bhwij,bhwje->bhwie', attn, bv2)
            return out.reshape(b, h, n, d)

        def attn_layer(x, Wqkv, qs, ksc, Wo):
            b, n, _ = x.shape
            qkv = x @ Wqkv
            q, k, v = jnp.split(qkv, 3, -1)
            sh = lambda t: t.reshape(b, n, HEADS, DIM_HEAD).transpose(0, 2, 1, 3)
            q, k, v = (sh(q), sh(k), sh(v))
            q = l2norm(q) * qs
            k = l2norm(k) * ksc
            freqs, scale = rotary_tables(n)
            cos, sin = (jnp.cos(freqs), jnp.sin(freqs))
            q = q * cos * scale + rotate_half(q) * sin * scale
            inv = 1.0 / scale
            k = k * cos * inv + rotate_half(k) * sin * inv
            out = local_attention(q, k, v)
            out = out.transpose(0, 2, 1, 3).reshape(b, n, INNER)
            return out @ Wo

        def ffn_layer(x, g, bln, W1, b1, W2, b2):
            mu = x.mean(-1, keepdims=True)
            var = ((x - mu) ** 2).mean(-1, keepdims=True)
            xn = (x - mu) / jnp.sqrt(var + 1e-05) * g + bln
            hg = xn @ W1 + b1
            a, gate = jnp.split(hg, 2, -1)
            return a * jax.nn.gelu(gate, approximate=False) @ W2 + b2
        key = jax.random.key(seed)
        ks = jax.random.split(key, 8)
        B, N = (2, 256)
        init = lambda k, shape: jax.random.normal(k, shape, jnp.float32) * 0.02
        return {'x': jax.random.normal(ks[0], (B, N, DIM), jnp.float32), 'Wqkv': init(ks[1], (DEPTH, DIM, 3 * INNER)), 'q_scale': jnp.ones((DEPTH, DIM_HEAD), jnp.float32), 'k_scale': jnp.ones((DEPTH, DIM_HEAD), jnp.float32), 'Wo': init(ks[2], (DEPTH, INNER, DIM)), 'ln_g': jnp.ones((DEPTH, DIM), jnp.float32), 'ln_b': jnp.zeros((DEPTH, DIM), jnp.float32), 'W1': init(ks[3], (DEPTH, DIM, 2 * DIM_INNER)), 'b1': jnp.zeros((DEPTH, 2 * DIM_INNER), jnp.float32), 'W2': init(ks[4], (DEPTH, DIM_INNER, DIM)), 'b2': jnp.zeros((DEPTH, DIM), jnp.float32)}
    _L0_ffn_in = _L0_ffn_setup()
    _L0_c = _w((lambda *s: np.random.randn(*s).astype(np.float32) * 0.05)(8, 128))
    _L0_wmod = _w((lambda *s: np.random.randn(*s).astype(np.float32) * 0.05)(128, 6 * 128) * 128 ** (-0.5))
    _d = {'L0_attn_x': _L0_attn_in['x'], 'L0_attn_Wq': _L0_attn_in['Wq'], 'L0_attn_Wk': _L0_attn_in['Wk'], 'L0_attn_Wv': _L0_attn_in['Wv'], 'L0_attn_Wo': _L0_attn_in['Wo'], 'L0_attn_bo': _L0_attn_in['bo'], 'L0_ffn_Wqkv': _L0_ffn_in['Wqkv'], 'L0_ffn_q_scale': _L0_ffn_in['q_scale'], 'L0_ffn_k_scale': _L0_ffn_in['k_scale'], 'L0_ffn_Wo': _L0_ffn_in['Wo'], 'L0_ffn_ln_g': _L0_ffn_in['ln_g'], 'L0_ffn_ln_b': _L0_ffn_in['ln_b'], 'L0_ffn_W1': _L0_ffn_in['W1'], 'L0_ffn_b1': _L0_ffn_in['b1'], 'L0_ffn_W2': _L0_ffn_in['W2'], 'L0_ffn_b2': _L0_ffn_in['b2'], 'L0_c': _L0_c, 'L0_wmod': _L0_wmod}
    _x0 = _d['L0_attn_x']
    _d['L0_attn_x'] = jax.random.normal(jax.random.fold_in(jax.random.key(seed), 1), (8, 512, 128), dtype=_x0.dtype)
    del _x0
    return _d

def reference(L0_attn_x, L0_attn_Wq, L0_attn_Wk, L0_attn_Wv, L0_attn_Wo, L0_attn_bo, L0_ffn_Wqkv, L0_ffn_q_scale, L0_ffn_k_scale, L0_ffn_Wo, L0_ffn_ln_g, L0_ffn_ln_b, L0_ffn_W1, L0_ffn_b1, L0_ffn_W2, L0_ffn_b2, L0_c, L0_wmod):

    def _L0_attn_ref(x, Wq, Wk, Wv, Wo, bo):
        import jax, jax.numpy as jnp
        import numpy as np
        DIM = 128
        HEADS = 16
        HEAD_DIM = 64
        N, S, _ = x.shape
        scale = 1.0 / np.sqrt(HEAD_DIM).astype(np.float32)
        q = (x @ Wq).reshape(N, S, HEADS, HEAD_DIM).transpose(0, 2, 1, 3)
        k = (x @ Wk).reshape(N, S, HEADS, HEAD_DIM).transpose(0, 2, 1, 3)
        v = (x @ Wv).reshape(N, S, HEADS, HEAD_DIM).transpose(0, 2, 1, 3)
        logits = jnp.einsum('nhid,nhjd->nhij', q, k) * scale
        causal = 1000000000.0 * (jnp.tril(jnp.ones((S, S), dtype=logits.dtype)) - 1.0)
        logits = logits + causal[None, None, :, :]
        attn = jax.nn.softmax(logits, axis=-1)
        out = jnp.einsum('nhij,nhjd->nhid', attn, v)
        out = out.transpose(0, 2, 1, 3).reshape(N, S, HEADS * HEAD_DIM)
        return out @ Wo + bo

    def _L0_ffn_ref(x, Wqkv, q_scale, k_scale, Wo, ln_g, ln_b, W1, b1, W2, b2):
        import jax, jax.numpy as jnp
        import numpy as np
        DIM = 128
        DEPTH = 6
        HEADS = 16
        DIM_HEAD = 64
        WINDOW = 32
        INNER = HEADS * DIM_HEAD
        DIM_INNER = int(DIM * 4 * 2 / 3)
        QK_SCALE = 8.0

        def shift_tokens(t):
            a, s = jnp.split(t, 2, -1)
            s = jnp.pad(s, ((0, 0), (1, 0), (0, 0)))[:, :-1]
            return jnp.concatenate([a, s], -1)

        def l2norm(t):
            return t / jnp.maximum(jnp.linalg.norm(t, axis=-1, keepdims=True), 1e-12)

        def rotate_half(x):
            x1, x2 = jnp.split(x, 2, -1)
            return jnp.concatenate([-x2, x1], -1)

        def rotary_tables(n):
            half = jnp.arange(0, DIM_HEAD, 2, dtype=jnp.float32)
            inv_freq = 1.0 / 10000.0 ** (half / DIM_HEAD)
            t = jnp.arange(n, dtype=jnp.float32)
            freqs = t[:, None] * inv_freq[None, :]
            freqs = jnp.concatenate([freqs, freqs], -1)
            base_scale = (half + 0.4 * DIM_HEAD) / (1.4 * DIM_HEAD)
            power = (t - n // 2) / (WINDOW // 2)
            scale = base_scale[None, :] ** power[:, None]
            scale = jnp.concatenate([scale, scale], -1)
            return (freqs, scale)

        def local_attention(q, k, v):
            b, h, n, d = q.shape
            w = WINDOW
            nw = n // w
            bq = q.reshape(b, h, nw, w, d)
            bk = k.reshape(b, h, nw, w, d)
            bv = v.reshape(b, h, nw, w, d)

            def look(t):
                p = jnp.pad(t, ((0, 0), (0, 0), (1, 0), (0, 0), (0, 0)))
                return jnp.concatenate([p[:, :, :nw], p[:, :, 1:]], axis=3)
            bk2, bv2 = (look(bk), look(bv))
            seq = jnp.arange(n).reshape(nw, w)
            seq_p = jnp.pad(seq, ((1, 0), (0, 0)), constant_values=-1)
            jt = jnp.concatenate([seq_p[:nw], seq_p[1:]], axis=1)
            it = seq[:, :, None]
            jb = jt[:, None, :]
            mask = (it < jb) | (it > jb + w) | (jb == -1)
            sim = jnp.einsum('bhwie,bhwje->bhwij', bq, bk2) * QK_SCALE
            sim = jnp.where(mask, -jnp.finfo(sim.dtype).max, sim)
            attn = jax.nn.softmax(sim, -1)
            out = jnp.einsum('bhwij,bhwje->bhwie', attn, bv2)
            return out.reshape(b, h, n, d)

        def attn_layer(x, Wqkv, qs, ksc, Wo):
            b, n, _ = x.shape
            qkv = x @ Wqkv
            q, k, v = jnp.split(qkv, 3, -1)
            sh = lambda t: t.reshape(b, n, HEADS, DIM_HEAD).transpose(0, 2, 1, 3)
            q, k, v = (sh(q), sh(k), sh(v))
            q = l2norm(q) * qs
            k = l2norm(k) * ksc
            freqs, scale = rotary_tables(n)
            cos, sin = (jnp.cos(freqs), jnp.sin(freqs))
            q = q * cos * scale + rotate_half(q) * sin * scale
            inv = 1.0 / scale
            k = k * cos * inv + rotate_half(k) * sin * inv
            out = local_attention(q, k, v)
            out = out.transpose(0, 2, 1, 3).reshape(b, n, INNER)
            return out @ Wo

        def ffn_layer(x, g, bln, W1, b1, W2, b2):
            mu = x.mean(-1, keepdims=True)
            var = ((x - mu) ** 2).mean(-1, keepdims=True)
            xn = (x - mu) / jnp.sqrt(var + 1e-05) * g + bln
            hg = xn @ W1 + b1
            a, gate = jnp.split(hg, 2, -1)
            return a * jax.nn.gelu(gate, approximate=False) @ W2 + b2
        for i in range(DEPTH):
            x = attn_layer(shift_tokens(x), Wqkv[i], q_scale[i], k_scale[i], Wo[i]) + x
            x = ffn_layer(shift_tokens(x), ln_g[i], ln_b[i], W1[i], b1[i], W2[i], b2[i]) + x
        return x
    x = L0_attn_x
    mod = (_silu(L0_c) @ L0_wmod).reshape(L0_c.shape[0], 6, 1, -1)
    sa, ca, ga, sb, cb, gb = (mod[:, 0], mod[:, 1], mod[:, 2], mod[:, 3], mod[:, 4], mod[:, 5])
    ga = (2 * (ga >= 0) - 1) * jnp.maximum(jnp.abs(ga), 0.25)
    gb = (2 * (gb >= 0) - 1) * jnp.maximum(jnp.abs(gb), 0.25)
    h = _layernorm(x, axis=-1) * (1 + ca) + sa
    x = x + ga * _L0_attn_ref(h, L0_attn_Wq, L0_attn_Wk, L0_attn_Wv, L0_attn_Wo, L0_attn_bo)
    h = _layernorm(x, axis=-1) * (1 + cb) + sb
    x = x + gb * _L0_ffn_ref(h, L0_ffn_Wqkv, L0_ffn_q_scale, L0_ffn_k_scale, L0_ffn_Wo, L0_ffn_ln_g, L0_ffn_ln_b, L0_ffn_W1, L0_ffn_b1, L0_ffn_W2, L0_ffn_b2)
    return x

_drawn_inputs = setup_inputs


def setup_inputs(seed=0):
    import zlib

    import numpy as np

    out = dict(_drawn_inputs(seed))
    spreads = {'L0_ffn_q_scale': (1.0, 0.6),
     'L0_ffn_k_scale': (1.0, 0.6),
     'L0_ffn_ln_g': (1.0, 0.6),
     'L0_ffn_ln_b': (0.0, 0.8),
     'L0_ffn_b1': (0.0, 0.8),
     'L0_ffn_b2': (0.0, 0.657)}
    factors = {'L0_attn_Wq': 8.0,
     'L0_attn_Wk': 8.0,
     'L0_attn_Wv': 8.0,
     'L0_attn_Wo': 8.0,
     'L0_attn_bo': 8.0,
     'L0_ffn_W1': 7.418,
     'L0_ffn_W2': 7.286}
    for name, (base, spread) in spreads.items():
        noise = np.random.default_rng([zlib.crc32(name.encode()), seed]).standard_normal(out[name].shape)
        drawn = base * np.exp(spread * noise) if base else spread * noise
        out[name] = jnp.asarray(drawn.astype(out[name].dtype))
    for name, factor in factors.items():
        out[name] = (out[name] * factor).astype(out[name].dtype)
    return out
```

```python
from contextlib import ExitStack

import numpy as np

import concourse.bass as bass
from concourse import mybir

F32 = mybir.dt.float32
BF16 = mybir.dt.bfloat16
ALU = mybir.AluOpType
ACT = mybir.ActivationFunctionType
AXX = mybir.AxisListType.X

NB = 8
S = 512
D = 128
NH = 16
DH = 64
L = 6
W = 32
NT = S // 128
FF = 341
FP = [128, 128, FF - 256]
NEG = -1e30
LN2 = 0.6931471805599453
V_BO, V_LAYER, V_B1 = 0, 1, 5
V_COLS = 1 + L * 10


class Queue:

    def __init__(self, name, sem):
        self.name, self.sem, self.count, self.items, self.waited = name, sem, 0, [], {}

    def wait(self, *tokens):
        need = {}
        for t in tokens:
            if t is not None and t[1] > need.get(t[0], (None, 0))[1]:
                need[t[0]] = t
        for key, t in need.items():
            if self.waited.get(key, 0) < t[1]:
                self.waited[key] = t[1]
                self.items.append(("wait", t[2], t[1]))

    def do(self, fn, *tokens, signal=True):
        self.wait(*tokens)
        if signal:
            self.count += 1
            self.items.append(("do", fn, self.sem, 1))
            return (self.name, self.count, self.sem)
        self.items.append(("do", fn, None, 0))
        return None

    def dma(self, slot, out, in_, *tokens):
        self.wait(*tokens)
        slot.count += 16
        self.items.append(("do", lambda e: e.dma_start(out, in_), slot.sem, 16))
        return (slot.name, slot.count, slot.sem)

    def play(self, eng):
        for it in self.items:
            if it[0] == "wait":
                eng.wait_ge(it[1], it[2])
            else:
                ins = it[1](eng)
                if it[2] is not None:
                    ins.then_inc(it[2], it[3])


class Slot:

    def __init__(self, name, sem):
        self.name, self.sem, self.count = name, sem, 0


class Place:

    def __init__(self, ap):
        self.ap, self.free = ap, []


class Ring:
    def __init__(self, places):
        self.places, self.at = places, 0

    def take(self):
        p = self.places[self.at % len(self.places)]
        self.at += 1
        return p


def constants():
    f = np.float32
    pos = np.arange(S)
    half = np.arange(0, DH, 2, dtype=f)
    inv = (f(1.0) / np.power(f(10000.0), half / f(DH))).astype(f)
    freqs = (pos.astype(f)[:, None] * inv[None, :]).astype(f).astype(np.float64)
    base = ((half + f(0.4 * DH)) / f(1.4 * DH)).astype(f).astype(np.float64)
    scale = base[None, :] ** ((pos - S // 2) / (W // 2))[:, None]
    cos, sin = np.cos(freqs), np.sin(freqs)
    rows = []
    for s in (8.0 * scale, 1.0 / scale):
        rows.append((np.concatenate([cos * s, cos * s], -1), np.concatenate([-sin * s, sin * s], -1)))
    tab = np.zeros((2, 128, NT, 2, DH), f)
    for qk in range(2):
        for cs in range(2):
            tab[cs, :, :, qk, :] = rows[qk][cs].reshape(NT, 128, DH).transpose(1, 0, 2)
    p = np.arange(128)[:, None]
    r = np.arange(64)[None, :]
    pw = p % W
    ok = np.where(r < W, pw <= r, (r - W) <= pw)
    first = ok & ~((p < W) & (r < W))
    mp = np.where(ok, 0.0, NEG)
    mp0 = np.where(first, 0.0, NEG)
    maskp = np.stack([np.concatenate([np.tile(mp0, (1, 4)), np.tile(mp, (1, 4))], 1), np.tile(mp, (1, 8))], 1)
    j = np.arange(128)[:, None]
    i = np.arange(160)[None, :]
    maskt = np.tile(np.where((j <= i) & (i <= j + W), 0.0, NEG), (1, 2))
    q = np.arange(128)[:, None]
    k = np.arange(128)[None, :]
    maskaq = np.where(k <= q, 0.0, NEG)
    maskak = np.where(k >= q, 0.0, NEG)
    masks = np.concatenate([maskp.reshape(128, 1024), maskt, maskaq, maskak, np.eye(128)], 1).astype(f)
    sel = np.repeat(np.eye(8), 128, 1).astype(f)
    mats = np.concatenate([np.eye(128), np.eye(128) - 1.0 / 128, np.full((128, 128), 1.0 / 128)], 1).astype(f)
    return {"tab": tab.reshape(2, 128, NT * 2 * DH), "masks": masks, "sel": sel, "mats": mats}


def program(nc, xt, wqt, wkt, wv, wo, wqkv, wof, w1, w2, vecs, scl, ct, wmod, tab, masks, sel, mats, out):
    ctx = ExitStack()
    with ctx:
        def sb(name, shape, dt=F32):
            return ctx.enter_context(nc.sbuf_tensor(name, shape, dt))

        def sem(name):
            return ctx.enter_context(nc.semaphore(name))

        PE = Queue("pe", sem("s_pe"))
        AC = Queue("act", sem("s_act"))
        DV = Queue("dve", sem("s_dve"))
        GP = Queue("pool", sem("s_pool"))
        SP = Queue("sync", None)

        def slot(name):
            return Slot(name, sem("s_" + name))

        t_mats = sb("t_mats", [128, 384])
        ident, center, mean = t_mats[:, 0:128], t_mats[:, 128:256], t_mats[:, 256:384]
        t_masks = sb("t_masks", [128, 1024 + 320 + 384], BF16)
        maskp = [t_masks[:, 512 * n:512 * n + 512] for n in range(2)]
        maskt = t_masks[:, 1024:1344]
        maskaq, maskak, identb = (t_masks[:, 1344 + 128 * n:1472 + 128 * n] for n in range(3))
        t_sel = sb("t_sel", [8, 8 * 128], BF16)
        t_tab = [sb(f"t_tab{n}", [128, NT, 2, DH]) for n in range(2)]
        t_rot = [sb(f"t_rot{n}", [128, NT, 2, DH]) for n in range(2)]
        t_scl = sb("t_scl", [128, 2, DH])
        t_vec = sb("t_vec", [128, V_COLS])
        t_mod = sb("t_mod", [128, 6, NB])
        t_ct = sb("t_ct", [128, 3, NB])
        xb = sb("xb", [128, NB, S + 1])
        xn = sb("xn", [128, NB, S])
        wbig = sb("wbig", [128, 3 * 1024])
        wout = sb("wout", [128, 8, 128])
        w1r = sb("w1r", [128, 2 * FF])
        w2r = sb("w2r", [128, 3, 128])
        b1s = sb("b1s", [128, 6])

        class Ctx:
            pass

        C = []
        for n in range(2):
            c = Ctx()
            c.qt = [Place(sb(f"qt{n}{x}", [128, 4, W + S])) for x in "qk"]
            c.qh = [Place(sb(f"qh{n}{x}", [128, 4, W + S], BF16)) for x in "qk"]
            c.v = Place(sb(f"v{n}", [128, NT, 8, 65]))
            c.pt = Ring([Place(sb(f"pt{n}{i}", [128, 8 * 160])) for i in range(2)])
            c.wk = Ring([Place(sb(f"wk{n}{i}", [128, 512])) for i in range(6)])
            c.ot = Place(sb(f"ot{n}", [128, 4, S]))
            c.acc = Place(sb(f"acc{n}", [128, S]))
            c.ngm = Place(sb(f"ngm{n}", [8, S + W], BF16))
            c.sm = Ring([Place(sb(f"sm{n}{i}", [128, 32])) for i in range(12)])
            c.ps = Ring([Place(ctx.enter_context(nc.psum_tensor(f"ps{n}{i}", [128, 512], F32))) for i in range(4)])
            C.append(c)

        def mm(o, l, r, *tokens, start=True, stop=True, signal=False, **kw):
            return PE.do(lambda e: e.matmul(o, l, r, start=start, stop=stop, skip_group_check=True, **kw),
                         *tokens, signal=signal)

        def tr(o, i, idn, *tokens, signal=False):
            return PE.do(lambda e: e.transpose(o, i, idn), *tokens, signal=signal)

        def act(o, i, f, *tokens, **kw):
            return AC.do(lambda e: e.activation(o, i, f, **kw), *tokens)

        def tt(q, o, a, b, op, *tokens):
            return q.do(lambda e: e.tensor_tensor(o, a, b, op), *tokens)

        def ts(q, o, a, s1, s2, o0, o1, *tokens):
            if o1 is None:
                return q.do(lambda e: e.tensor_scalar(o, a, s1, None, o0), *tokens)
            return q.do(lambda e: e.tensor_scalar(o, a, s1, s2, o0, o1), *tokens)

        def copy(q, o, i, *tokens):
            return q.do(lambda e: e.tensor_copy(o, i), *tokens)

        def reduce(o, i, op, *tokens):
            return DV.do(lambda e: e.tensor_reduce(o, i, AXX, op), *tokens)

        def recip(o, i, *tokens):
            return DV.do(lambda e: e.reciprocal(o, i), *tokens)

        def fill(o, value, *tokens):
            return DV.do(lambda e: e.memset(o, value), *tokens)

        def stt(o, a, s, b, o0, o1, *tokens):
            return DV.do(lambda e: e.scalar_tensor_tensor(out=o, in0=a, scalar=s, in1=b, op0=o0, op1=o1), *tokens)

        s_c = slot("const")
        st_masks = C[0].qt[0].ap.rearrange("p a b -> p (a b)")[:, 0:1728]
        st_sel = C[1].qt[0].ap.rearrange("p a b -> p (a b)")[0:8, 0:1024]
        for o, i in ((t_mats[:, :], mats), (st_masks, masks), (st_sel, sel),
                     (t_tab[0][:, :, :, :].rearrange("p a b c -> p (a b c)"), tab[0]),
                     (t_tab[1][:, :, :, :].rearrange("p a b c -> p (a b c)"), tab[1]),
                     (t_vec[:, :], vecs), (t_ct[:, 0, :], ct)):
            const_in = SP.dma(s_c, o, i)
        s_x = slot("x")
        for b in range(NB):
            x_in = SP.dma(s_x, xb[:, b, 0:S], xt[b])
        s_wa = slot("wa")
        wqk_in = SP.dma(s_wa, wbig[:, 0:1024].rearrange("p (a c) -> p a c", a=8), wqt.rearrange("(a p) c -> p a c", p=128))
        wqk_in = SP.dma(s_wa, wbig[:, 1024:2048].rearrange("p (a c) -> p a c", a=8), wkt.rearrange("(a p) c -> p a c", p=128))
        wqk_in = wv_in = SP.dma(s_wa, wbig[:, 2048:3072], wv)
        s_wo = slot("wo")
        wo_in = SP.dma(s_wo, wout[:, :, :], wo.rearrange("(a p) c -> p a c", p=128))
        s_wm = slot("wm")
        wmod_t = xn[:, 0, :]
        wm_in = SP.dma(s_wm, xn[:, 0:2, 0:384], wmod.rearrange("p (a c) -> p a c", a=2))

        pads = [copy(DV, t_masks[:, :], st_masks, const_in), copy(DV, t_sel[:, :], st_sel)]
        t_eps = sb("t_eps", [128, 2])
        pads.append(fill(t_eps[:, 0:1], 1e-5, *pads))
        pads.append(fill(t_eps[:, 1:2], 10.0 * LN2))
        for c in C:
            for k in range(2):
                for t in (c.qt[k].ap, c.qh[k].ap):
                    pads.append(fill(t[:, :, S:S + W] if k == 0 else t[:, :, 0:W], 0.0))
            pads.append(fill(c.ngm.ap[:, S:S + W], 0.0))
            pads.append(fill(c.v.ap[:, :, :, 64:65], 1.0))
        ready = pads[-1]

        def tables(name):
            AC.do(lambda e: e.preload_act_table_set(name), signal=False)

        tables("natural_log_exp_and_others")

        ex = act(t_ct[:, 1, :], t_ct[:, 0, :], ACT.Exp, const_in, ready, scale=-1.0)
        a1 = ts(DV, t_ct[:, 1, :], t_ct[:, 1, :], 1.0, None, ALU.add, None, ex)
        a1 = recip(t_ct[:, 2, :], t_ct[:, 1, :], a1)
        silu = tt(DV, t_ct[:, 1, :], t_ct[:, 0, :], t_ct[:, 2, :], ALU.mult, a1)
        bank = C[0].ps.take()
        for j in range(6):
            pm = mm(bank.ap[:, 8 * j:8 * j + 8], xn[:, j // 3, 128 * (j % 3):128 * (j % 3) + 128], t_ct[:, 1, :],
                    silu, wm_in, start=(j == 0), stop=(j == 5), signal=True)
        mod = copy(DV, t_mod[:, :, :].rearrange("p a b -> p (a b)"), bank.ap[:, 0:48], pm)
        bank.free = [mod]
        for j in (1, 4):
            mod = ts(DV, t_mod[:, j, :], t_mod[:, j, :], 1.0, None, ALU.add, None, mod)
        for j in (2, 5):
            g = t_mod[:, j, :]
            m1 = ts(DV, t_ct[:, 0, :], g, 0.0, None, ALU.is_ge, None, mod)
            m1 = ts(DV, t_ct[:, 0, :], t_ct[:, 0, :], 2.0, -1.0, ALU.mult, ALU.add, m1)
            m2 = ts(DV, t_ct[:, 2, :], g, -1.0, None, ALU.mult, None, m1)
            m2 = tt(DV, t_ct[:, 2, :], t_ct[:, 2, :], g, ALU.max, m2)
            m2 = ts(DV, t_ct[:, 2, :], t_ct[:, 2, :], 0.25, None, ALU.max, None, m2)
            mod = tt(DV, g, t_ct[:, 0, :], t_ct[:, 2, :], ALU.mult, m2)
        mods = mod
        pm_wm = pm

        afold = xn[:, 4:8, :].rearrange("p a b -> p (a b)")
        fold = []
        for g in range(4):
            bank_e, bank_o = C[g % 2].ps.take(), C[g % 2].ps.take()
            for r in range(4):
                h = 4 * g + r
                bk = (bank_e, bank_o)[h % 2]
                rows = slice(64 * (h % 2), 64 * (h % 2) + 64)
                pm = mm(bk.ap[:, 128 * (r // 2):128 * (r // 2) + 128],
                        wbig[rows, 128 * (h // 2):128 * (h // 2) + 128],
                        wbig[rows, 1024 + 128 * (h // 2):1152 + 128 * (h // 2)], wqk_in, *bk.free,
                        signal=True)
            dst = afold[:, 512 * g:512 * g + 512].rearrange("p (a e c) -> p a e c", a=2, e=2)
            for e_, bk in enumerate((bank_e, bank_o)):
                f = act(dst[:, :, e_, :], bk.ap[:, 0:256].rearrange("p (a c) -> p a c", a=2), ACT.Copy, pm, scale=0.125)
                bk.free = [f]
            fold.append(f)
        fold = fold[-1]

        x_ready = {b: x_in for b in range(NB)}
        x_read = {b: [] for b in range(NB)}

        def rsqrt(c, src, dst, tmp, shift, *tokens):
            sc, bi = (2.0 ** 20, t_eps[:, 1:2]) if shift else (1.0, 0.0)
            a = act(tmp, src, ACT.Ln, *tokens, scale=sc)
            a = act(dst, tmp, ACT.Exp, a, scale=-0.5, bias=bi)
            d = tt(DV, tmp, dst, dst, ALU.mult, a)
            d = tt(DV, tmp, tmp, src, ALU.mult, d)
            d = ts(DV, tmp, tmp, -0.5, 1.5, ALU.mult, ALU.add, d)
            return tt(DV, dst, dst, tmp, ALU.mult, d)

        def layernorm(c, src, dst, t_src, *dst_free):
            pc, pv = c.ps.take(), c.ps.take()
            ctr = mm(pc.ap[:, :], center, src, t_src, *pc.free, signal=True)
            wq, wr, wt = c.wk.take(), c.wk.take(), c.wk.take()
            sq = act(wq.ap[:, :], pc.ap[:, :], ACT.Square, ctr, *wq.free)
            var = mm(pv.ap[:, :], mean, wq.ap[:, :], sq, *pv.free, signal=True)
            v = ts(DV, wr.ap[:, :], pv.ap[:, :], 1e-5, None, ALU.add, None, var, *wr.free)
            pv.free = [v]
            r = rsqrt(c, wr.ap[:, :], wq.ap[:, :], wt.ap[:, :], False, v, *wt.free)
            done = tt(DV, dst, pc.ap[:, :], wq.ap[:, :], ALU.mult, r, *dst_free)
            pc.free, wq.free, wr.free, wt.free = [done, sq], [done], [done], [done]
            return done, ctr

        def finish_heads(c, half, o_place, t, o_done):
            bank = c.ps.take()
            for i in range(4):
                p = tr(bank.ap[:, 128 * i:128 * i + 128], o_place.ap[:, 128 * i:128 * i + 128], ident,
                       o_done, *bank.free, signal=(i == 3))
            o_place.free = [p]
            e = act(c.ot.ap[:, :, 128 * t:128 * t + 128], bank.ap[:, :].rearrange("p (a b) -> p a b", a=4), ACT.Copy,
                    p, *c.ot.free)
            bank.free = [e]
            return e

        def project_out(c, b, half, ot_done, w_in, emit):
            bank = c.ps.take()
            for i in range(4):
                p = mm(bank.ap[:, :], wout[:, 4 * half + i, :], c.ot.ap[:, i, :], ot_done, w_in, *bank.free,
                       start=(i == 0), stop=(i == 3), signal=(i == 3))
            c.ot.free = [p]
            if half == 0:
                a = act(c.acc.ap[:, :], bank.ap[:, :], ACT.Copy, p, *c.acc.free)
                bank.free = [a]
                c.acc_done = a
                return p
            s = tt(DV, c.acc.ap[:, :], bank.ap[:, :], c.acc.ap[:, :], ALU.add, p, c.acc_done)
            bank.free = [s]
            c.acc.free = [emit(s)]
            return p

        def v_chunk(c, src, t, wcols, t_src, w_in):
            bank = c.ps.take()
            p = mm(bank.ap[:, :], src[:, 128 * t:128 * t + 128], wbig[:, wcols:wcols + 512], t_src, w_in, *bank.free,
                   signal=True)
            v = act(c.v.ap[:, t, :, 0:64], bank.ap[:, :].rearrange("p (h d) -> p h d", h=8), ACT.Copy,
                    p, ready, *c.v.free)
            bank.free = [v]
            return p, v

        def causal(c, b):
            ht, hh = c.qt[1].ap[:, 0, 0:S], c.qh[1].ap[:, 0, 0:S]
            done, read = layernorm(c, xb[:, b, 0:S], ht, x_ready[b], *c.qt[1].free, *c.qh[1].free)
            hdone = ts(DV, ht, ht, t_mod[:, 1, b:b + 1], t_mod[:, 0, b:b + 1], ALU.mult, ALU.add, done, mods)
            hcast = copy(DV, hh, ht, hdone)
            yield
            last = None
            for half in range(2):
                for t in range(NT):
                    p, v_done = v_chunk(c, ht, t, 2048 + 512 * half, hdone, wv_in)
                c.v.free = []
                yield
                o_half = c.obig
                for g in range(2):
                    yt, yh = c.qt[0].ap, c.qh[0].ap
                    for r in range(4):
                        h = 8 * half + 4 * g + r
                        bank = c.ps.take()
                        p = mm(bank.ap[:, :], afold[:, 128 * h:128 * h + 128], ht, hdone, fold, *bank.free, signal=True)
                        y1 = act(yt[:, r, 0:S], bank.ap[:, :], ACT.Copy, p, *c.qt[0].free)
                        y2 = copy(DV, yh[:, r, 0:S], yt[:, r, 0:S], y1, *c.qh[0].free)
                        bank.free = [y1]
                    c.qt[0].free, c.qh[0].free = [], []
                    yield
                    m = c.sm.take()
                    for i in range(NT):
                        for r in range(4):
                            bank = c.ps.take()
                            n = 128 * (i + 1)
                            mm(bank.ap[:, 0:n], yh[:, r, 128 * i:128 * i + 128], hh[:, 0:n], y2, hcast, *bank.free,
                               start=True, stop=False)
                            p = mm(bank.ap[:, n - 128:n], identb, maskaq, start=False, stop=True, signal=True)
                            mx = reduce(m.ap[:, 4 * i + r:4 * i + r + 1], bank.ap[:, 0:n], ALU.max, p, *m.free)
                            bank.free = [mx]
                        yield
                    c.qh[0].free = [p]
                    bank = c.ps.take()
                    for i in range(NT):
                        p = tr(bank.ap[0:4, 128 * i:128 * i + 128], m.ap[:, 4 * i:4 * i + 4], ident, mx, *bank.free,
                               signal=(i == NT - 1))
                    m.free = [p]
                    ng = act(c.ngm.ap[0:4, 0:S], bank.ap[0:4, :], ACT.Copy, p, *c.ngm.free, scale=-1.0)
                    bank.free = [ng]
                    yield
                    for r in range(4):
                        h8 = 4 * g + r
                        pt = c.pt.take()
                        off = 0
                        offs = []
                        for j in range(NT):
                            n = S - 128 * j
                            bank = c.ps.take()
                            mm(bank.ap[:, 0:n], ht[:, 128 * j:128 * j + 128], yt[:, r, 128 * j:S], y1, hdone,
                               *bank.free, start=True, stop=False)
                            mm(bank.ap[:, 0:n], t_sel[0:4, 128 * r:128 * r + 128], c.ngm.ap[0:4, 128 * j:S], ng,
                               start=False, stop=False)
                            p = mm(bank.ap[:, 0:128], identb, maskak, start=False, stop=True, signal=True)
                            ex = act(pt.ap[:, off:off + n], bank.ap[:, 0:n], ACT.Exp, p, *pt.free)
                            bank.free = [ex]
                            offs.append(off)
                            off += n
                        yield
                        bank = c.ps.take()
                        first = True
                        for i in range(NT):
                            for j in range(i + 1):
                                at = offs[j] + 128 * (i - j)
                                p = mm(bank.ap[:, 65 * i:65 * i + 65], pt.ap[:, at:at + 128], c.v.ap[:, j, h8, :],
                                       ex, v_done, *bank.free, start=first, stop=(i == NT - 1 and j == i),
                                       signal=(i == NT - 1 and j == i))
                                first = False
                        pt.free = [p]
                        rc = c.sm.take()
                        pv = bank.ap[:, 0:260].rearrange("p (a b) -> p a b", a=4)
                        d = recip(rc.ap[:, 0:4], pv[:, :, 64], p, *rc.free)
                        o = tt(DV, o_half.ap[:, :, 64 * r:64 * r + 64], pv[:, :, 0:64],
                               rc.ap[:, 0:4].unsqueeze(2).to_broadcast([128, 4, 64]), ALU.mult, d, *o_half.free, mods, pm_wm)
                        rc.free = [o]
                        bank.free = [o]
                        yield
                    c.qt[0].free = [p]
                    c.ngm.free = [p]
                    c.v.free = [p]
                    for tp in range(2):
                        bank = c.ps.take()
                        for y in range(4):
                            t, i = 2 * tp + y // 2, y % 2
                            p = tr(bank.ap[:, 128 * y:128 * y + 128], o_half.ap[:, t, 128 * i:128 * i + 128], ident, o,
                                   *bank.free, signal=(y == 3))
                        e = act(c.ot.ap[:, 2 * g:2 * g + 2, 256 * tp:256 * tp + 256].rearrange(
                            "p a (t n) -> p t a n", t=2), bank.ap[:, :].rearrange("p (t a n) -> p t a n", t=2, a=2),
                            ACT.Copy, p, *c.ot.free)
                        bank.free = [e]
                    o_half.free = [p]
                c.ot.free = []
                yield

                def emit(s):
                    z = ts(DV, c.acc.ap[:, :], c.acc.ap[:, :], t_vec[:, V_BO:V_BO + 1], t_mod[:, 2, b:b + 1],
                           ALU.add, ALU.mult, s)
                    z = tt(DV, xb[:, b, 0:S], xb[:, b, 0:S], c.acc.ap[:, :], ALU.add, z, read)
                    c.x1 = z
                    return z
                last = project_out(c, b, half, e, wo_in, emit)
                yield
            c.qt[1].free, c.qh[1].free = [last], [last]
            x1 = c.x1
            wp = c.wk.take()
            keep = SP.dma(s_x1[b], x1d[b], xb[:, b, 0:S], x1)
            done, read = layernorm(c, xb[:, b, 0:S], wp.ap[:, :], x1, *wp.free)
            z = fill(xb[64:128, b, 0:1], 0.0, read, keep)
            a = ts(DV, xb[0:64, b, 0:S], wp.ap[0:64, :], t_mod[0:64, 4, b:b + 1], t_mod[0:64, 3, b:b + 1],
                   ALU.mult, ALU.add, done, keep)
            a2 = ts(DV, xb[64:128, b, 1:S + 1], wp.ap[64:128, :], t_mod[64:128, 4, b:b + 1],
                    t_mod[64:128, 3, b:b + 1], ALU.mult, ALU.add, done, z)
            wp.free = [a2]
            x_ready[b] = a2
            kept[b] = keep
            yield

        def local(c, b, li):
            src = xb[:, b, :]
            xt_ = x_ready[b]
            for half in range(2):
                for k in range(2):
                    col = 1024 * k + 512 * half
                    for t in range(NT):
                        bank = c.ps.take()
                        p = mm(bank.ap[:, :], src[:, 128 * t:128 * t + 128], wbig[:, col:col + 512], xt_, c.w_in,
                               *bank.free, signal=True)
                        wn, wu, ww = c.wk.take(), c.wk.take(), c.wk.take()
                        s1, s2, s3 = c.sm.take(), c.sm.take(), c.sm.take()
                        sq = act(ww.ap[:, :], bank.ap[:, :], ACT.Square, p, *ww.free)
                        ss = reduce(s1.ap[:, 0:8], ww.ap[:, :].rearrange("p (h d) -> p h d", h=8), ALU.add, sq, *s1.free)
                        ss = ts(DV, s1.ap[:, 0:8], s1.ap[:, 0:8], 1e-24, None, ALU.max, None, ss)
                        rn = rsqrt(c, s1.ap[:, 0:8], s2.ap[:, 0:8], s3.ap[:, 0:8], True, ss, *s2.free, *s3.free)
                        q3 = lambda a: a.rearrange("p (h d) -> p h d", h=8)
                        n = tt(DV, q3(wn.ap[:, :]), q3(bank.ap[:, :]),
                               s2.ap[:, 0:8].unsqueeze(2).to_broadcast([128, 8, 64]), ALU.mult, rn, *wn.free)
                        bank.free = [n, sq]
                        for s_ in (s1, s2, s3):
                            s_.free = [n]
                        u = tt(DV, q3(wu.ap[:, :]), q3(wn.ap[:, :]),
                               t_rot[0][:, t, k, :].unsqueeze(1).to_broadcast([128, 8, 64]), ALU.mult,
                               n, c.rot, *wu.free)
                        q4 = lambda a: a.rearrange("p (h e d) -> p h e d", h=8, e=2)
                        v = n
                        for e_ in range(2):
                            v = tt(GP, q4(ww.ap[:, :])[:, :, e_, :], q4(wn.ap[:, :])[:, :, 1 - e_, :],
                                   t_rot[1][:, t, k, 32 * e_:32 * e_ + 32].unsqueeze(1).to_broadcast([128, 8, 32]),
                                   ALU.mult, v, ss, c.rot, n)
                        w_ = tt(GP, wu.ap[:, :], wu.ap[:, :], ww.ap[:, :], ALU.add, v, u)
                        wn.free, ww.free = [u, v], [w_]
                        yield
                        bank = c.ps.take()
                        for i in range(4):
                            p = tr(bank.ap[:, 128 * i:128 * i + 128], wu.ap[:, 128 * i:128 * i + 128], ident, w_,
                                   *bank.free, signal=(i == 3))
                        wu.free = [p]
                        o = W if k else 0
                        b3 = bank.ap[:, :].rearrange("p (a b) -> p a b", a=4)
                        e1 = act(c.qt[k].ap[:, :, o + 128 * t:o + 128 * t + 128], b3, ACT.Copy, p, ready, *c.qt[k].free)
                        e2 = copy(DV, c.qh[k].ap[:, :, o + 128 * t:o + 128 * t + 128],
                                  c.qt[k].ap[:, :, o + 128 * t:o + 128 * t + 128], e1, ready, *c.qh[k].free)
                        bank.free = [e1]
                    c.qt[k].free, c.qh[k].free = [], []
                qk32, qk16 = e1, e2
                for t in range(NT):
                    p, v_done = v_chunk(c, src, t, 2048 + 512 * half, xt_, c.w_in)
                c.v.free = []
                x_read[b] = [p]
                yield
                m = c.sm.take()
                for tp in range(2):
                    be, bo = c.ps.take(), c.ps.take()
                    for bk in (be, bo):
                        mm(bk.ap[:, :], identb, maskp[tp], *bk.free, start=True, stop=False)
                    for tq in range(2):
                        t = 2 * tp + tq
                        for i in range(4):
                            for e_, bk in enumerate((be, bo)):
                                rows = slice(64 * e_, 64 * e_ + 64)
                                for g in range(4):
                                    o = 256 * tq + 64 * i
                                    last = tq == 1 and i == 3 and g == 3
                                    p = mm(bk.ap[32 * g:32 * g + 32, o:o + 64],
                                           c.qh[0].ap[rows, i, 128 * t + 32 * g:128 * t + 32 * g + 32],
                                           c.qh[1].ap[rows, i, 128 * t + 32 * g:128 * t + 32 * g + 64], qk16,
                                           start=False, stop=last, signal=last,
                                           tile_position=(64 * e_, 32 * g))
                    for e_, bk in enumerate((be, bo)):
                        mx = reduce(m.ap[:, 16 * tp:16 * tp + 16].rearrange("p (t e i) -> p t e i", t=2, e=2)[:, :, e_, :],
                                    bk.ap[:, :].rearrange("p (t i r) -> p t i r", t=2, i=4), ALU.max, p, *m.free)
                        bk.free = [mx]
                    yield
                c.qh[0].free, c.qh[1].free = [p], [p]
                bank = c.ps.take()
                for t in range(NT):
                    p = tr(bank.ap[0:8, 128 * t:128 * t + 128], m.ap[:, 8 * t:8 * t + 8], ident, mx, *bank.free,
                           signal=(t == NT - 1))
                m.free = [p]
                ng = act(c.ngm.ap[:, 0:S], bank.ap[0:8, :], ACT.Copy, p, *c.ngm.free, scale=-1.0)
                bank.free = [ng]
                yield
                prev = None
                for t in range(NT):
                    pt = c.pt.take()
                    exps = {}
                    for pair in range(2):
                        banks = (c.ps.take(), c.ps.take())
                        for bk in banks:
                            mm(bk.ap[:, 0:320], identb, maskt, *bk.free, start=True, stop=False)
                        for e_, bk in enumerate(banks):
                            for y in range(2):
                                r = 4 * e_ + 2 * pair + y
                                mm(bk.ap[:, 160 * y:160 * y + 160], t_sel[0:8, 128 * r:128 * r + 128],
                                   c.ngm.ap[:, 128 * t:128 * t + 160], ng, start=False, stop=False)
                        for y in range(2):
                            for e_, bk in enumerate(banks):
                                rows = slice(64 * e_, 64 * e_ + 64)
                                i = 2 * pair + y
                                p = mm(bk.ap[:, 160 * y:160 * y + 160],
                                       c.qt[1].ap[rows, i, W + 128 * t:W + 128 * t + 128],
                                       c.qt[0].ap[rows, i, 128 * t:128 * t + 160], qk32,
                                       start=False, stop=(y == 1), signal=(y == 1))
                        for e_, bk in enumerate(banks):
                            r = 4 * e_ + 2 * pair
                            ex = act(pt.ap[:, 160 * r:160 * r + 320], bk.ap[:, 0:320], ACT.Exp, p, *pt.free)
                            bk.free = [ex]
                        yield
                    banks = (c.ps.take(), c.ps.take())
                    for e_, bk in enumerate(banks):
                        for i in range(4):
                            r = 4 * e_ + i
                            h8 = 2 * i + e_
                            p = mm(bk.ap[:, 65 * i:65 * i + 65], pt.ap[:, 160 * r:160 * r + 128],
                                   c.v.ap[:, t, h8, :], ex, v_done, *bk.free, start=(i == 0),
                                   stop=(i == 3), signal=(i == 3))
                    if prev is not None:
                        for e_, bk in enumerate(banks):
                            for i in range(4):
                                r = 4 * e_ + i
                                h8 = 2 * i + e_
                                p = mm(bk.ap[0:32, 65 * i:65 * i + 65],
                                       prev.ap[96:128, 160 * r + 128:160 * r + 160], c.v.ap[96:128, t - 1, h8, :],
                                       start=False, stop=(i == 3), signal=(i == 3), tile_position=(96, 0))
                        prev.free = [p]
                    prev = pt
                    wo_ = c.wk.take()
                    for e_, bk in enumerate(banks):
                        rc = c.sm.take()
                        pv = bk.ap[:, 0:260].rearrange("p (a b) -> p a b", a=4)
                        d = recip(rc.ap[:, 0:4], pv[:, :, 64], p, *rc.free)
                        o = tt(DV, wo_.ap[:, :].rearrange("p (i e d) -> p i e d", i=4, e=2)[:, :, e_, :], pv[:, :, 0:64],
                               rc.ap[:, 0:4].unsqueeze(2).to_broadcast([128, 4, 64]), ALU.mult, d, *wo_.free)
                        rc.free = [o]
                        bk.free = [o]
                    yield
                    e = finish_heads(c, half, wo_, t, o)
                prev.free = [p]
                c.qt[0].free, c.qt[1].free, c.ngm.free, c.v.free = [p], [p], [p], [p]
                c.ot.free = []

                def emit(s):
                    a = tt(DV, xb[0:64, b, 0:S], xb[0:64, b, 0:S], c.acc.ap[0:64, :], ALU.add, s, xt_, *x_read[b])
                    a = tt(DV, xb[64:128, b, 1:S + 1], xb[64:128, b, 1:S + 1], c.acc.ap[64:128, :], ALU.add, s)
                    c.x1 = a
                    return a
                last = project_out(c, b, half, e, c.wo_in, emit)
                wo_read.append(last)
                yield
            done, read = layernorm(c, xb[:, b, 0:S], xn[:, b, :], c.x1, *xn_free[b])
            x_ready[b], x_read[b] = c.x1, [read]
            xn_ready[b] = done
            yield

        def feed(c, b, li):
            us = []
            for j in range(3):
                n = FP[j]
                ba, bg = c.ps.take(), c.ps.take()
                mm(ba.ap[0:n, :], w1r[:, 128 * j:128 * j + n], xn[:, b, :], xn_ready[b], c.w1_in, *ba.free)
                p = mm(bg.ap[0:n, :], w1r[:, FF + 128 * j:FF + 128 * j + n], xn[:, b, :], *bg.free, signal=True)
                g, u = c.wk.take(), c.wk.take()
                ge = act(g.ap[0:n, :], bg.ap[0:n, :], ACT.Gelu, p, c.b1_in, *g.free, bias=b1s[0:n, 3 + j:4 + j])
                ud = stt(u.ap[0:n, :], ba.ap[0:n, :], b1s[0:n, j:j + 1], g.ap[0:n, :], ALU.add, ALU.mult, ge, *u.free)
                bg.free, ba.free, g.free = [ge], [ud], [ud]
                us.append((u, ud))
                yield
            xn_free[b] = [p]
            bank = c.ps.take()
            for j in range(3):
                n = FP[j]
                p = mm(bank.ap[:, :], w2r[0:n, j, :], us[j][0].ap[0:n, :], us[j][1], c.w2_in, *bank.free,
                       start=(j == 0), stop=(j == 2), signal=(j == 2))
                us[j][0].free = [p]
            us[0][0].free = us[1][0].free = us[2][0].free = [p]
            w2_read.append(p)
            b2 = t_vec[:, V_LAYER + 10 * li + 2:V_LAYER + 10 * li + 3]
            a = stt(xb[0:64, b, 0:S], bank.ap[0:64, :], b2[0:64, :], xb[0:64, b, 0:S], ALU.add, ALU.add, p,
                    x_ready[b], *x_read[b])
            a = stt(xb[64:128, b, 1:S + 1], bank.ap[64:128, :], b2[64:128, :], xb[64:128, b, 1:S + 1],
                    ALU.add, ALU.add, p)
            bank.free = [a]
            x_ready[b] = a
            x_read[b] = []
            yield

        def together(works):
            live = [(lambda ws: (y for w in ws for y in w))(ws) for ws in works]
            step = 0
            while live:
                for g in list(live):
                    try:
                        next(g)
                    except StopIteration:
                        live.remove(g)

        s_x1 = [slot(f"x1_{b}") for b in range(NB)]
        x1d = nc.dram_tensor("x1_keep", [NB, 128, S], F32).ap()
        kept = {}
        xn_free = {b: [] for b in range(NB)}
        xn_ready = {}
        for n, c in enumerate(C):
            c.n = n
            c.obig = Place(xn[:, 2 * n:2 * n + 2, :].rearrange("p a (b d) -> p (a b) d", b=2))
        together([[causal(C[n], b) for b in range(n, NB, 2)] for n in range(2)])
        fold_read = [PE_last for PE_last in [(PE.name, PE.count, PE.sem)]]
        for b in range(NB):
            xn_free[b] = list(fold_read)

        s_w1, s_w2, s_scl = slot("w1"), slot("w2"), slot("scl")
        wo_read, w2_read = [], []
        rot = None
        b1d = None
        for li in range(L):
            big_free = fold_read if li == 0 else qkv_read
            w_in = SP.dma(s_wa, wbig[:, :], wqkv[li], *big_free)
            wo_in2 = SP.dma(s_wo, wout[:, :, :], wof[li].rearrange("(a p) c -> p a c", p=128), *big_free)
            scl_in = SP.dma(s_scl, t_scl[:, :, :].rearrange("p a b -> p (a b)"), scl[li], rot)
            w1_in = SP.dma(s_w1, w1r[:, :], w1[li], *w2_read, b1d)
            for j in range(3):
                w2_in = SP.dma(s_w2, w2r[0:FP[j], j, :], w2[li, 128 * j:128 * j + FP[j], :], *w2_read)
            r1 = tt(GP, t_rot[0][:, :, :, :], t_tab[0][:, :, :, :],
                    t_scl[:, :, :].unsqueeze(1).to_broadcast([128, NT, 2, DH]), ALU.mult, scl_in, const_in, *big_free)
            for e_ in range(2):
                rot = tt(GP, t_rot[1][:, :, :, 32 * e_:32 * e_ + 32], t_tab[1][:, :, :, 32 * e_:32 * e_ + 32],
                         t_scl[:, :, 32 * (1 - e_):32 * (1 - e_) + 32].unsqueeze(1).to_broadcast([128, NT, 2, 32]),
                         ALU.mult, r1)
            bank = C[0].ps.take()
            vl = V_LAYER + 10 * li
            for k in range(2):
                for j in range(3):
                    n = FP[j]
                    pb = mm(bank.ap[0:n, 3 * k + j:3 * k + j + 1], w1r[:, FF * k + 128 * j:FF * k + 128 * j + n],
                            t_vec[:, vl + 1:vl + 2], w1_in, *bank.free, start=(k == 0 and j == 0), stop=True,
                            signal=True)
            for k in range(2):
                tt(DV, b1s[:, 3 * k:3 * k + 2], bank.ap[:, 3 * k:3 * k + 2], t_vec[:, vl + 4 + 3 * k:vl + 6 + 3 * k],
                   ALU.add, pb, *w2_read)
                b1d = tt(DV, b1s[0:FP[2], 3 * k + 2:3 * k + 3], bank.ap[0:FP[2], 3 * k + 2:3 * k + 3],
                         t_vec[0:FP[2], vl + 6 + 3 * k:vl + 7 + 3 * k], ALU.add)
            bank.free = [b1d]
            w1s = ts(DV, w1r[:, :], w1r[:, :], t_vec[:, vl:vl + 1], None, ALU.mult, None, b1d)
            for c in C:
                c.w_in, c.wo_in, c.rot, c.w1_in, c.b1_in, c.w2_in = w_in, wo_in2, rot, w1s, b1d, w2_in
            wo_read.clear()
            tables("natural_log_exp_and_others")
            together([[local(C[n], b, li) for b in range(n, NB, 2)] for n in range(2)])
            tables("gelu_and_others")
            qkv_read = [(PE.name, PE.count, PE.sem), (GP.name, GP.count, GP.sem), (DV.name, DV.count, DV.sem)]
            w2_read.clear()
            together([[feed(C[n], b, li) for b in range(n, NB, 2)] for n in range(2)])
            b1d = w2_read[-1]

        s_out, s_x1r = slot("out"), slot("x1r")
        for b in range(NB):
            back = SP.dma(s_x1r, xn[:, b, :], x1d[b], kept[b], *xn_free[b])
        for b in range(NB):
            z = stt(xn[0:64, b, :], xb[0:64, b, 0:S], t_mod[0:64, 5, b:b + 1], xn[0:64, b, :], ALU.mult, ALU.add,
                    back, x_ready[b])
            z = stt(xn[64:128, b, :], xb[64:128, b, 1:S + 1], t_mod[64:128, 5, b:b + 1], xn[64:128, b, :],
                    ALU.mult, ALU.add)
            o = SP.dma(s_out, out[b], xn[:, b, :], z)
        SP.wait(o)

        block = ctx.enter_context(nc.Block())

        @block.sync
        def _(e):
            SP.play(e)

        @block.tensor
        def _(e):
            PE.play(e)

        @block.scalar
        def _(e):
            AC.play(e)

        @block.vector
        def _(e):
            DV.play(e)

        @block.gpsimd
        def _(e):
            GP.play(e)


def kernel(**inputs):
    import concourse.bacc as _bacc
    from concourse.bass_utils import run_bass_kernel_spmd as _run

    a = {k: np.asarray(v) for k, v in inputs.items()}
    f = np.float32
    vecs = np.zeros((128, V_COLS), f)
    vecs[:, V_BO] = a["L0_attn_bo"]
    for li in range(L):
        o = V_LAYER + 10 * li
        vecs[:, o] = a["L0_ffn_ln_g"][li]
        vecs[:, o + 1] = a["L0_ffn_ln_b"][li]
        vecs[:, o + 2] = a["L0_ffn_b2"][li]
        for k in range(2):
            for j in range(3):
                vecs[0:FP[j], o + 4 + 3 * k + j] = a["L0_ffn_b1"][li][FF * k + 128 * j:FF * k + 128 * j + FP[j]]
    scl = np.concatenate([a["L0_ffn_q_scale"], a["L0_ffn_k_scale"]], 1)
    arrays = {
        "xt": a["L0_attn_x"].transpose(0, 2, 1),
        "wqt": a["L0_attn_Wq"].T, "wkt": a["L0_attn_Wk"].T, "wv": a["L0_attn_Wv"], "wo": a["L0_attn_Wo"],
        "wqkv": a["L0_ffn_Wqkv"], "wof": a["L0_ffn_Wo"], "w1": a["L0_ffn_W1"], "w2": a["L0_ffn_W2"],
        "vecs": vecs, "scl": np.broadcast_to(scl[:, None, :], (L, 128, 2 * DH)), "ct": a["L0_c"].T, "wmod": a["L0_wmod"],
    }
    arrays.update(constants())
    arrays = {k: np.ascontiguousarray(v) for k, v in arrays.items()}
    nc = _bacc.Bacc("TRN2", target_bir_lowering=False, num_devices=1)
    args = {k: nc.dram_tensor(k, v.shape, mybir.dt.from_np(v.dtype), kind="ExternalInput").ap() for k, v in arrays.items()}
    args["out"] = nc.dram_tensor("out", (NB, 128, S), F32, kind="ExternalOutput").ap()
    program(nc, **args)
    r = _run(nc, [arrays], core_ids=[0])
    return r.results[0]["out"].transpose(0, 2, 1)
```

```python
from contextlib import ExitStack

import numpy as np

import concourse.bass as bass
from concourse import mybir

F32 = mybir.dt.float32
BF16 = mybir.dt.bfloat16
F16 = mybir.dt.float16
ALU = mybir.AluOpType
ACT = mybir.ActivationFunctionType
AXX = mybir.AxisListType.X

NB = 8
S = 512
D = 128
NH = 16
DH = 64
L = 6
W = 32
NT = S // 128
FF = 341
FP = [128, 128, FF - 256]
NEG = -1e30
LN2 = 0.6931471805599453
WK = 8
WS = 64.0
LAG = 1
V_BO, V_LAYER, V_B1 = 0, 1, 5
V_COLS = 1 + L * 10


class Queue:

    def __init__(self, name, sem):
        self.name, self.sem, self.count, self.items, self.waited = name, sem, 0, [], {}

    def wait(self, *tokens):
        need = {}
        for t in tokens:
            if t is not None and t[1] > need.get(t[0], (None, 0))[1]:
                need[t[0]] = t
        for key, t in need.items():
            if self.waited.get(key, 0) < t[1]:
                self.waited[key] = t[1]
                self.items.append(("wait", t[2], t[1]))

    def do(self, fn, *tokens, signal=True):
        self.wait(*tokens)
        if signal:
            self.count += 1
            self.items.append(("do", fn, self.sem, 1))
            return (self.name, self.count, self.sem)
        self.items.append(("do", fn, None, 0))
        return None

    def dma(self, slot, out, in_, *tokens):
        self.wait(*tokens)
        slot.count += 16
        self.items.append(("do", lambda e: e.dma_start(out, in_), slot.sem, 16))
        return (slot.name, slot.count, slot.sem)

    def play(self, eng):
        for it in self.items:
            if it[0] == "wait":
                eng.wait_ge(it[1], it[2])
            else:
                ins = it[1](eng)
                if it[2] is not None:
                    ins.then_inc(it[2], it[3])


class Slot:

    def __init__(self, name, sem):
        self.name, self.sem, self.count = name, sem, 0


class Place:

    def __init__(self, ap):
        self.ap, self.free = ap, []


class Ring:
    def __init__(self, places):
        self.places, self.at = places, 0

    def take(self):
        p = self.places[self.at % len(self.places)]
        self.at += 1
        return p


def constants():
    f = np.float32
    pos = np.arange(S)
    half = np.arange(0, DH, 2, dtype=f)
    inv = (f(1.0) / np.power(f(10000.0), half / f(DH))).astype(f)
    freqs = (pos.astype(f)[:, None] * inv[None, :]).astype(f).astype(np.float64)
    base = ((half + f(0.4 * DH)) / f(1.4 * DH)).astype(f).astype(np.float64)
    scale = base[None, :] ** ((pos - S // 2) / (W // 2))[:, None]
    cos, sin = np.cos(freqs), np.sin(freqs)
    rows = []
    for s in (8.0 * scale, 1.0 / scale):
        rows.append((np.concatenate([cos * s, cos * s], -1), np.concatenate([-sin * s, sin * s], -1)))
    tab = np.zeros((2, 128, NT, 2, DH), f)
    for qk in range(2):
        for cs in range(2):
            tab[cs, :, :, qk, :] = rows[qk][cs].reshape(NT, 128, DH).transpose(1, 0, 2)
    p = np.arange(128)[:, None]
    r = np.arange(64)[None, :]
    pw = p % W
    ok = np.where(r < W, pw <= r, (r - W) <= pw)
    first = ok & ~((p < W) & (r < W))
    mp = np.where(ok, 0.0, NEG)
    mp0 = np.where(first, 0.0, NEG)
    maskp = np.stack([np.concatenate([np.tile(mp0, (1, 4)), np.tile(mp, (1, 4))], 1), np.tile(mp, (1, 8))], 1)
    left = np.zeros((104, 8, 128), f)
    right = np.zeros((104, 160), f)
    key, qry = np.arange(128), np.arange(160)
    left[32 * ((key // W) % 2) + key % W, :, key] = 1.0
    left[64 + key // W, :, key] = 1.0
    for r in range(8):
        left[96 + r, r, :] = 1.0
    for r in range(64):
        same = (qry // W) % 2 == r // 32
        right[r] = np.where(np.where(same, r % 32 > qry % W, r % 32 < qry % W), NEG, 0.0)
    for w in range(4):
        right[64 + w] = np.where((qry // W - w == 0) | (qry // W - w == 1), 0.0, NEG)
    q = np.arange(128)[:, None]
    k = np.arange(128)[None, :]
    maskaq = np.where(k <= q, 0.0, NEG)
    maskak = np.where(k >= q, 0.0, NEG)
    masks = np.concatenate([maskp.reshape(128, 1024), maskaq, maskak, np.eye(128)], 1).astype(f)
    mats = np.concatenate([np.eye(128), np.eye(128) - 1.0 / 128, np.full((128, 128), 1.0 / 128)], 1).astype(f)
    return {"tab": tab.reshape(2, 128, NT * 2 * DH), "masks": masks, "left": left.reshape(104, 1024), "right": right, "mats": mats}


def program(nc, xt, wqt, wkt, wv, wo, wqkv, wof, w1, w2, vecs, scl, ct, wmod, tab, masks, left, right, mats, out):
    ctx = ExitStack()
    with ctx:
        def sb(name, shape, dt=F32):
            return ctx.enter_context(nc.sbuf_tensor(name, shape, dt))

        def sem(name):
            return ctx.enter_context(nc.semaphore(name))

        PE = Queue("pe", sem("s_pe"))
        AC = Queue("act", sem("s_act"))
        DV = Queue("dve", sem("s_dve"))
        GP = Queue("pool", sem("s_pool"))
        SP = Queue("sync", None)

        def slot(name):
            return Slot(name, sem("s_" + name))

        t_mats = sb("t_mats", [128, 384])
        ident, center, mean = t_mats[:, 0:128], t_mats[:, 128:256], t_mats[:, 256:384]
        t_masks = sb("t_masks", [128, 1024 + 384], BF16)
        maskp = [t_masks[:, 512 * n:512 * n + 512] for n in range(2)]
        maskaq, maskak, identb = (t_masks[:, 1024 + 128 * n:1152 + 128 * n] for n in range(3))
        t_left = sb("t_left", [104, 8 * 128], BF16)
        t_rots = sb("t_rots", [128, 2, NT * 2 * DH])
        t_rot = [t_rots[:, n, :].rearrange("p (t k d) -> p t k d", t=NT, k=2) for n in range(2)]
        t_scl = sb("t_scl", [128, 2, DH])
        t_vec = sb("t_vec", [128, V_COLS])
        t_mod = sb("t_mod", [128, 6, NB])
        t_ct = sb("t_ct", [128, 3, NB])
        xb = sb("xb", [128, NB, S + 1])
        wbig = sb("wbig", [128, 3 * 1024])
        wsplit = wbig[:, :].bitcast(F16)
        wstage = Ring([Place(sb(f"wstage{i}", [128, 512])) for i in range(2)])
        wout = sb("wout", [128, 8, 128])
        w12 = sb("w12", [128, 2 * FF + 3 * 128])
        w1r = w12[:, 0:2 * FF]
        w2r = w12[:, 2 * FF:2 * FF + 384].rearrange("p (a b) -> p a b", a=3)
        b1s = sb("b1s", [128, 6])

        class Ctx:
            pass

        C = []
        for n in range(2):
            c = Ctx()
            c.qt = [Place(sb(f"qt{n}{x}", [128, 4, W + S])) for x in "qk"]
            c.qh = [Place(sb(f"qh{n}{x}", [128, 4, W + S], BF16)) for x in "qk"]
            c.v = Place(sb(f"v{n}", [128, 2, NT, 8, 65], F16))
            c.pt = Ring([Place(sb(f"pt{n}{i}", [128, 2, 8 * 160], F16)) for i in range(3)])
            c.wk = Ring([Place(sb(f"wk{n}{i}", [128, 512])) for i in range(WK)])
            c.ot = Place(sb(f"ot{n}", [128, 4, 256]))
            c.acc = Place(sb(f"acc{n}", [128, S]))
            c.xs = Place(sb(f"xs{n}", [128, 2, S], F16))
            c.rhs = Place(sb(f"rhs{n}", [104, NT, 160], BF16))
            c.sm = Ring([Place(sb(f"sm{n}{i}", [128, 32])) for i in range(12)])
            c.ps = Ring([Place(ctx.enter_context(nc.psum_tensor(f"ps{n}{i}", [128, 512], F32))) for i in range(4)])
            C.append(c)

        work = [0.0]

        def mm(o, l, r, *tokens, start=True, stop=True, signal=False, **kw):
            n = r.shape[-1] if len(r.shape) == 2 else int(np.prod(r.shape[1:]))
            work[0] += max(256, 4 * n) if l.dtype == F32 else max(64, n)
            return PE.do(lambda e: e.matmul(o, l, r, start=start, stop=stop, skip_group_check=True, **kw),
                         *tokens, signal=signal)

        def mm3(o, l, r, *tokens, start=True, stop=True, signal=False, **kw):
            mm(o, l[0], r[1], *tokens, start=start, stop=False, **kw)
            mm(o, l[1], r[0], start=False, stop=False, **kw)
            return mm(o, l[0], r[0], start=False, stop=stop, signal=signal, **kw)

        def tr(o, i, idn, *tokens, signal=False):
            work[0] += 128
            return PE.do(lambda e: e.transpose(o, i, idn), *tokens, signal=signal)

        def act(o, i, f, *tokens, **kw):
            return AC.do(lambda e: e.activation(o, i, f, **kw), *tokens)

        def tt(q, o, a, b, op, *tokens):
            return q.do(lambda e: e.tensor_tensor(o, a, b, op), *tokens)

        def ts(q, o, a, s1, s2, o0, o1, *tokens):
            if o1 is None:
                return q.do(lambda e: e.tensor_scalar(o, a, s1, None, o0), *tokens)
            return q.do(lambda e: e.tensor_scalar(o, a, s1, s2, o0, o1), *tokens)

        def copy(q, o, i, *tokens):
            return q.do(lambda e: e.tensor_copy(o, i), *tokens)

        def reduce(o, i, op, *tokens):
            return DV.do(lambda e: e.tensor_reduce(o, i, AXX, op), *tokens)

        def recip(o, i, *tokens):
            return DV.do(lambda e: e.reciprocal(o, i), *tokens)

        def fill(o, value, *tokens):
            return DV.do(lambda e: e.memset(o, value), *tokens)

        def stt(o, a, s, b, o0, o1, *tokens):
            return DV.do(lambda e: e.scalar_tensor_tensor(out=o, in0=a, scalar=s, in1=b, op0=o0, op1=o1), *tokens)

        s_c = slot("const")
        st_masks = C[0].qt[0].ap.rearrange("p a b -> p (a b)")[:, 0:1408]
        st_left = C[1].qt[0].ap.rearrange("p a b -> p (a b)")[0:104, 0:1024]
        st_right = C[1].qt[0].ap.rearrange("p a b -> p (a b)")[0:104, 1024:1184]
        for o, i in ((t_mats[:, :], mats), (st_masks, masks), (st_left, left), (st_right, right),
                     (t_vec[:, :], vecs), (t_ct[:, 0, :], ct)):
            const_in = SP.dma(s_c, o, i)
        s_x = slot("x")
        for b in range(NB):
            x_in = SP.dma(s_x, xb[:, b, 0:S], xt[b])
        s_wa = slot("wa")
        wqk_in = SP.dma(s_wa, wbig[:, 0:1024].rearrange("p (a c) -> p a c", a=8), wqt.rearrange("(a p) c -> p a c", p=128))
        wqk_in = SP.dma(s_wa, wbig[:, 1024:2048].rearrange("p (a c) -> p a c", a=8), wkt.rearrange("(a p) c -> p a c", p=128))
        wqk_in = wv_in = SP.dma(s_wa, wbig[:, 2048:3072], wv)
        s_wo = slot("wo")
        wo_in = SP.dma(s_wo, wout[:, :, :], wo.rearrange("(a p) c -> p a c", p=128))
        s_wm = slot("wm")
        t_wmod = C[0].pt.places[0].ap.rearrange("p a b -> p (a b)").bitcast(F32)[:, 0:768]
        wm_in = SP.dma(s_wm, t_wmod, wmod)

        pads = [copy(DV, t_masks[:, :], st_masks, const_in), copy(DV, t_left[:, :], st_left)]
        for c in C:
            for t in range(NT):
                pads.append(copy(DV, c.rhs.ap[:, t, :], st_right))
        t_eps = sb("t_eps", [128, 2])
        pads.append(fill(t_eps[:, 0:1], 1e-5, *pads))
        pads.append(fill(t_eps[:, 1:2], 10.0 * LN2))
        for c in C:
            for k in range(2):
                for t in (c.qt[k].ap, c.qh[k].ap):
                    pads.append(fill(t[:, :, S:S + W] if k == 0 else t[:, :, 0:W], 0.0, pads[-1]))
            pads.append(fill(c.v.ap[:, 0, :, :, 64:65], 1.0))
            pads.append(fill(c.v.ap[:, 1, :, :, 64:65], 0.0))
        ready = pads[-1]

        def tables(name):
            AC.do(lambda e: e.preload_act_table_set(name), signal=False)

        tables("natural_log_exp_and_others")

        ex = act(t_ct[:, 1, :], t_ct[:, 0, :], ACT.Exp, const_in, ready, scale=-1.0)
        a1 = ts(DV, t_ct[:, 1, :], t_ct[:, 1, :], 1.0, None, ALU.add, None, ex)
        a1 = recip(t_ct[:, 2, :], t_ct[:, 1, :], a1)
        silu = tt(DV, t_ct[:, 1, :], t_ct[:, 0, :], t_ct[:, 2, :], ALU.mult, a1)
        bank = C[0].ps.take()
        for j in range(6):
            pm = mm(bank.ap[:, 8 * j:8 * j + 8], t_wmod[:, 128 * j:128 * j + 128], t_ct[:, 1, :],
                    silu, wm_in, start=(j == 0), stop=(j == 5), signal=True)
        mod = copy(DV, t_mod[:, :, :].rearrange("p a b -> p (a b)"), bank.ap[:, 0:48], pm)
        bank.free = [mod]
        for j in (1, 4):
            mod = ts(DV, t_mod[:, j, :], t_mod[:, j, :], 1.0, None, ALU.add, None, mod)
        for j in (2, 5):
            g = t_mod[:, j, :]
            m1 = ts(DV, t_ct[:, 0, :], g, 0.0, None, ALU.is_ge, None, mod)
            m1 = ts(DV, t_ct[:, 0, :], t_ct[:, 0, :], 2.0, -1.0, ALU.mult, ALU.add, m1)
            m2 = ts(DV, t_ct[:, 2, :], g, -1.0, None, ALU.mult, None, m1)
            m2 = tt(DV, t_ct[:, 2, :], t_ct[:, 2, :], g, ALU.max, m2)
            m2 = ts(DV, t_ct[:, 2, :], t_ct[:, 2, :], 0.25, None, ALU.max, None, m2)
            mod = tt(DV, g, t_ct[:, 0, :], t_ct[:, 2, :], ALU.mult, m2)
        mods = mod
        C[0].pt.places[0].free = [pm]

        afold = [t_rots[:, :, :].rearrange("p a b -> p (a b)"), w12[:, 0:1024]]
        fold = []
        for g in range(4):
            bank_e, bank_o = C[g % 2].ps.take(), C[g % 2].ps.take()
            for r in range(4):
                h = 4 * g + r
                bk = (bank_e, bank_o)[h % 2]
                rows = slice(64 * (h % 2), 64 * (h % 2) + 64)
                pm = mm(bk.ap[:, 128 * (r // 2):128 * (r // 2) + 128],
                        wbig[rows, 128 * (h // 2):128 * (h // 2) + 128],
                        wbig[rows, 1024 + 128 * (h // 2):1152 + 128 * (h // 2)], wqk_in, *bk.free,
                        signal=True)
            dst = afold[g // 2][:, 512 * (g % 2):512 * (g % 2) + 512].rearrange("p (a e c) -> p a e c", a=2, e=2)
            for e_, bk in enumerate((bank_e, bank_o)):
                f = act(dst[:, :, e_, :], bk.ap[:, 0:256].rearrange("p (a c) -> p a c", a=2), ACT.Copy, pm, scale=0.125)
                bk.free = [f]
            fold.append(f)
        fold = fold[-1]

        x_ready = {b: x_in for b in range(NB)}
        x_read = {b: [] for b in range(NB)}

        def rsqrt(c, src, dst, tmp, shift, *tokens):
            sc, bi = (2.0 ** 20, t_eps[:, 1:2]) if shift else (1.0, 0.0)
            a = act(tmp, src, ACT.Ln, *tokens, scale=sc)
            a = act(dst, tmp, ACT.Exp, a, scale=-0.5, bias=bi)
            d = tt(DV, tmp, dst, dst, ALU.mult, a)
            d = tt(DV, tmp, tmp, src, ALU.mult, d)
            d = ts(DV, tmp, tmp, -0.5, 1.5, ALU.mult, ALU.add, d)
            return tt(DV, dst, dst, tmp, ALU.mult, d)

        def layernorm(c, src, dst, t_src, *dst_free):
            pc, pv = c.ps.take(), c.ps.take()
            ctr = mm(pc.ap[:, :], center, src, t_src, *pc.free, signal=True)
            wq, wr, wt = c.wk.take(), c.wk.take(), c.wk.take()
            sq = act(wq.ap[:, :], pc.ap[:, :], ACT.Square, ctr, *wq.free)
            var = mm(pv.ap[:, :], mean, wq.ap[:, :], sq, *pv.free, signal=True)
            v = ts(DV, wr.ap[:, :], pv.ap[:, :], 1e-5, None, ALU.add, None, var, *wr.free)
            pv.free = [v]
            r = rsqrt(c, wr.ap[:, :], wq.ap[:, :], wt.ap[:, :], False, v, *wt.free)
            done = tt(DV, dst, pc.ap[:, :], wq.ap[:, :], ALU.mult, r, *dst_free)
            pc.free, wq.free, wr.free, wt.free = [done, sq], [done], [done], [done]
            return done, ctr

        def finish_heads(c, half, o_place, t, o_done):
            bank = c.ps.take()
            for i in range(4):
                p = tr(bank.ap[:, 128 * i:128 * i + 128], o_place.ap[:, 128 * i:128 * i + 128], ident,
                       o_done, *bank.free, signal=(i == 3))
            o_place.free = [p]
            e = act(c.ot.ap[:, :, 128 * (t % 2):128 * (t % 2) + 128], bank.ap[:, :].rearrange("p (a b) -> p a b", a=4), ACT.Copy,
                    p, *c.ot.free)
            bank.free = [e]
            return e

        def project_out(c, half, tp, ot_done, w_in):
            bank = c.ps.take()
            for i in range(4):
                p = mm(bank.ap[:, 0:256], wout[:, 4 * half + i, :], c.ot.ap[:, i, :], ot_done, w_in, *bank.free,
                       start=(i == 0), stop=(i == 3), signal=(i == 3))
            c.ot.free = [p]
            a = c.acc.ap[:, 256 * tp:256 * tp + 256]
            if half == 0:
                done = act(a, bank.ap[:, 0:256], ACT.Copy, p, *c.acc.free)
                c.acc_done = done
            else:
                done = tt(DV, a, bank.ap[:, 0:256], a, ALU.add, p, c.acc_done)
            bank.free = [done]
            return p, done

        def v_chunk(c, l, r, scale, *tokens):
            bank, t = c.ps.take(), c.vt
            c.vt = (c.vt + 1) % NT
            if isinstance(l, tuple):
                p = mm3(bank.ap[:, :], l, r, *tokens, *bank.free, signal=True)
            else:
                p = mm(bank.ap[:, :], l, r, *tokens, *bank.free, signal=True)
            b3 = bank.ap[:, :].rearrange("p (h d) -> p h d", h=8)
            v = act(c.v.ap[:, 0, t, :, 0:64], b3, ACT.Copy, p, ready, *c.v.free, scale=scale)
            v = stt(c.v.ap[:, 1, t, :, 0:64], b3, scale, c.v.ap[:, 0, t, :, 0:64], ALU.mult, ALU.subtract, v)
            bank.free = [v]
            return p, v

        def exp_split(c, bank, n, pt, off, p):
            w_ = c.wk.take()
            ex = act(w_.ap[:, 0:n], bank.ap[:, 0:n], ACT.Exp, p, *w_.free)
            bank.free = [ex]
            hi = copy(DV, pt.ap[:, 0, off:off + n], w_.ap[:, 0:n], ex, *pt.free)
            lo = tt(GP, pt.ap[:, 1, off:off + n], w_.ap[:, 0:n], pt.ap[:, 0, off:off + n], ALU.subtract, hi)
            w_.free = [lo]
            return lo

        def causal(c, b):
            ht, hh = c.qt[1].ap[:, 0, 0:S], c.qh[1].ap[:, 0, 0:S]
            ngm_a = c.rhs.ap[96:100, :, :].rearrange("p a b -> p (a b)")[:, 0:S]
            sel_a = t_left[96:100, :]
            done, read = layernorm(c, xb[:, b, 0:S], ht, x_ready[b], *c.qt[1].free, *c.qh[1].free)
            hdone = ts(DV, ht, ht, t_mod[:, 1, b:b + 1], t_mod[:, 0, b:b + 1], ALU.mult, ALU.add, done, mods)
            hcast = copy(DV, hh, ht, hdone)
            yield
            last = None
            for half in range(2):
                for t in range(NT):
                    p, v_done = v_chunk(c, ht[:, 128 * t:128 * t + 128], wbig[:, 2048 + 512 * half:2560 + 512 * half],
                                        1.0, hdone, wv_in)
                    yield
                c.v.free = []
                o_half = c.obig
                for g in range(2):
                    yt, yh = c.qt[0].ap, c.qh[0].ap
                    for r in range(4):
                        h = 8 * half + 4 * g + r
                        bank = c.ps.take()
                        p = mm(bank.ap[:, :], afold[half][:, 128 * (h % 8):128 * (h % 8) + 128], ht, hdone, fold, *bank.free, signal=True)
                        y1 = act(yt[:, r, 0:S], bank.ap[:, :], ACT.Copy, p, *c.qt[0].free)
                        y2 = copy(DV, yh[:, r, 0:S], yt[:, r, 0:S], y1, *c.qh[0].free)
                        bank.free = [y1]
                        yield
                    c.qt[0].free, c.qh[0].free = [], []
                    yield
                    m = c.sm.take()
                    for i in range(NT):
                        for r in range(4):
                            bank = c.ps.take()
                            n = 128 * (i + 1)
                            mm(bank.ap[:, 0:n], yh[:, r, 128 * i:128 * i + 128], hh[:, 0:n], y2, hcast, *bank.free,
                               start=True, stop=False)
                            p = mm(bank.ap[:, n - 128:n], identb, maskaq, start=False, stop=True, signal=True)
                            mx = reduce(m.ap[:, 4 * i + r:4 * i + r + 1], bank.ap[:, 0:n], ALU.max, p, *m.free)
                            bank.free = [mx]
                        yield
                    c.qh[0].free = [p]
                    bank = c.ps.take()
                    for i in range(NT):
                        p = tr(bank.ap[0:4, 128 * i:128 * i + 128], m.ap[:, 4 * i:4 * i + 4], ident, mx, *bank.free,
                               signal=(i == NT - 1))
                    m.free = [p]
                    ng = act(ngm_a[:, :], bank.ap[0:4, :], ACT.Copy, p, *c.rhs.free, scale=-1.0)
                    bank.free = [ng]
                    yield
                    offs = [0, 512, 896, 1152]
                    pts = {}

                    def scores(r):
                        pt = pts[r] = c.pt.take()
                        for j in range(NT):
                            n = S - 128 * j
                            bank = c.ps.take()
                            mm(bank.ap[:, 0:n], ht[:, 128 * j:128 * j + 128], yt[:, r, 128 * j:S], y1, hdone,
                               *bank.free, start=True, stop=False)
                            mm(bank.ap[:, 0:n], sel_a[:, 128 * r:128 * r + 128], ngm_a[:, 128 * j:S], ng,
                               start=False, stop=False)
                            p = mm(bank.ap[:, 0:128], identb, maskak, start=False, stop=True, signal=True)
                            ex = exp_split(c, bank, n, pt, offs[j], p)
                            yield
                        pts[r] = (pt, ex)

                    def values(r):
                        h8 = 4 * g + r
                        pt, ex = pts[r]
                        bank = c.ps.take()
                        first = True
                        for i in range(NT):
                            for j in range(i + 1):
                                at = offs[j] + 128 * (i - j)
                                p = mm3(bank.ap[:, 65 * i:65 * i + 65],
                                        (pt.ap[:, 0, at:at + 128], pt.ap[:, 1, at:at + 128]),
                                        (c.v.ap[:, 0, j, h8, :], c.v.ap[:, 1, j, h8, :]),
                                        ex, v_done, *bank.free, start=first, stop=(i == NT - 1 and j == i),
                                        signal=(i == NT - 1 and j == i))
                                first = False
                        pt.free = [p]
                        rc = c.sm.take()
                        pv = bank.ap[:, 0:260].rearrange("p (a b) -> p a b", a=4)
                        d = recip(rc.ap[:, 0:4], pv[:, :, 64], p, *rc.free)
                        o = tt(DV, o_half.ap[:, :, 64 * r:64 * r + 64], pv[:, :, 0:64],
                               rc.ap[:, 0:4].unsqueeze(2).to_broadcast([128, 4, 64]), ALU.mult, d, *o_half.free, mods)
                        rc.free = [o]
                        bank.free = [o]
                        return p, o

                    for r in range(5):
                        if r < 4:
                            yield from scores(r)
                        if r > 0:
                            p, o = values(r - 1)
                            yield
                    c.qt[0].free = [p]
                    c.rhs.free = [p]
                    c.v.free = [p]
                    for tp in range(2):
                        bank = c.ps.take()
                        for y in range(4):
                            t, i = 2 * tp + y // 2, y % 2
                            p = tr(bank.ap[:, 128 * y:128 * y + 128], o_half.ap[:, t, 128 * i:128 * i + 128], ident, o,
                                   *bank.free, signal=(y == 3))
                        ot = c.ot.ap[:, 2 * tp:2 * tp + 2, :].rearrange("p a n -> p (a n)")
                        e = act(ot.rearrange("p (i t n) -> p t i n", i=2, t=2),
                                bank.ap[:, :].rearrange("p (t i n) -> p t i n", t=2, i=2), ACT.Copy, p, *c.ot.free)
                        bank.free = [e]
                    o_half.free = [p]
                    c.ot.free = []
                    yield
                    for tp in range(2):
                        bank = c.ps.take()
                        for i in range(2):
                            p = mm(bank.ap[:, 0:256], wout[:, 4 * half + 2 * g + i, :], c.ot.ap[:, 2 * tp + i, :],
                                   e, wo_in, *bank.free, start=(i == 0), stop=(i == 1), signal=(i == 1))
                        a = c.acc.ap[:, 256 * tp:256 * tp + 256]
                        if half == 0 and g == 0:
                            done = act(a, bank.ap[:, 0:256], ACT.Copy, p, *c.acc.free)
                            first_acc = done
                        else:
                            done = tt(DV, a, bank.ap[:, 0:256], a, ALU.add, p, first_acc, last)
                        bank.free = [done]
                    last = done
                    c.ot.free = [p]
                    yield
            z = ts(DV, c.acc.ap[:, :], c.acc.ap[:, :], t_vec[:, V_BO:V_BO + 1], t_mod[:, 2, b:b + 1],
                   ALU.add, ALU.mult, last)
            c.x1 = tt(DV, xb[:, b, 0:S], xb[:, b, 0:S], c.acc.ap[:, :], ALU.add, z, read)
            c.acc.free = [c.x1]
            last = p
            c.qt[1].free, c.qh[1].free = [last], [last]
            x1 = c.x1
            wp = c.wk.take()
            keep = SP.dma(s_x1[b], x1d[b], xb[:, b, 0:S], x1)
            done, read = layernorm(c, xb[:, b, 0:S], wp.ap[:, :], x1, *wp.free)
            z = fill(xb[64:128, b, 0:1], 0.0, read, keep)
            a = ts(DV, xb[0:64, b, 0:S], wp.ap[0:64, :], t_mod[0:64, 4, b:b + 1], t_mod[0:64, 3, b:b + 1],
                   ALU.mult, ALU.add, done, keep)
            a2 = ts(DV, xb[64:128, b, 1:S + 1], wp.ap[64:128, :], t_mod[64:128, 4, b:b + 1],
                    t_mod[64:128, 3, b:b + 1], ALU.mult, ALU.add, done, z)
            wp.free = [a2]
            x_ready[b] = a2
            kept[b] = keep
            yield

        def local(c, b, li):
            src = xb[:, b, :]
            xt_ = x_ready[b]
            xh = copy(DV, c.xs.ap[:, 0, :], src[:, 0:S], xt_, *c.xs.free)
            xs = tt(DV, c.xs.ap[:, 1, :], src[:, 0:S], c.xs.ap[:, 0, :], ALU.subtract, xh)
            yield

            def x_of(t):
                return tuple(c.xs.ap[:, z, 128 * t:128 * t + 128] for z in range(2))

            def w_of(col):
                return tuple(wsplit[:, 3072 * z + col:3072 * z + col + 512] for z in range(2))

            q3 = lambda a: a.rearrange("p (h d) -> p h d", h=8)
            q4 = lambda a: a.rearrange("p (h e d) -> p h e d", h=8, e=2)

            def rotate(half, k, t):
                bank = c.ps.take()
                p = mm3(bank.ap[:, :], x_of(t), w_of(1024 * k + 512 * half), xs, c.w_in, *bank.free, signal=True)
                wn, wu, ww = c.wk.take(), c.wk.take(), c.wk.take()
                s1, s2, s3 = c.sm.take(), c.sm.take(), c.sm.take()
                sq = act(ww.ap[:, :], bank.ap[:, :], ACT.Square, p, *ww.free)
                ss = reduce(s1.ap[:, 0:8], q3(ww.ap[:, :]), ALU.add, sq, *s1.free)
                ss = ts(DV, s1.ap[:, 0:8], s1.ap[:, 0:8], WS * WS * 1e-24, None, ALU.max, None, ss)
                rn = rsqrt(c, s1.ap[:, 0:8], s2.ap[:, 0:8], s3.ap[:, 0:8], True, ss, *s2.free, *s3.free)
                n = tt(DV, q3(wn.ap[:, :]), q3(bank.ap[:, :]), s2.ap[:, 0:8].unsqueeze(2).to_broadcast([128, 8, 64]),
                       ALU.mult, rn, *wn.free)
                bank.free = [n]
                for s_ in (s1, s2, s3):
                    s_.free = [n]
                u = tt(DV, q3(wu.ap[:, :]), q3(wn.ap[:, :]),
                       t_rot[0][:, t, k, :].unsqueeze(1).to_broadcast([128, 8, 64]), ALU.mult, n, c.rot, *wu.free)
                v = n
                for e_ in range(2):
                    v = tt(GP, q4(ww.ap[:, :])[:, :, e_, :], q4(wn.ap[:, :])[:, :, 1 - e_, :],
                           t_rot[1][:, t, k, 32 * e_:32 * e_ + 32].unsqueeze(1).to_broadcast([128, 8, 32]),
                           ALU.mult, v, n, c.rot)
                w_ = tt(GP, wu.ap[:, :], wu.ap[:, :], ww.ap[:, :], ALU.add, v, u)
                wn.free, ww.free = [u, v], [w_]
                return wu, w_

            def turn(k, t, wu, w_):
                bank = c.ps.take()
                for i in range(4):
                    p = tr(bank.ap[:, 128 * i:128 * i + 128], wu.ap[:, 128 * i:128 * i + 128], ident, w_,
                           *bank.free, signal=(i == 3))
                wu.free = [p]
                o = (W if k else 0) + 128 * t
                e1 = act(c.qt[k].ap[:, :, o:o + 128], bank.ap[:, :].rearrange("p (a b) -> p a b", a=4), ACT.Copy,
                         p, ready, *c.qt[k].free)
                bank.free = [e1]
                return e1, copy(DV, c.qh[k].ap[:, :, o:o + 128], c.qt[k].ap[:, :, o:o + 128], e1, ready, *c.qh[k].free)

            for half in range(2):
                chunks = [(k, t) for t in range(NT) for k in range(2)]
                made = []
                for n in range(len(chunks) + LAG):
                    if n < len(chunks):
                        made.append(rotate(half, *chunks[n]))
                        yield
                    if n % 2 == 0 and n // 2 < NT:
                        p, v_done = v_chunk(c, x_of(n // 2), w_of(2048 + 512 * half), 1.0 / WS, xs, c.w_in)
                        yield
                    if n >= LAG:
                        qk32, qk16 = turn(*chunks[n - LAG], *made[n - LAG])
                        yield
                for k in range(2):
                    c.qt[k].free, c.qh[k].free = [], []
                c.v.free = []
                if half:
                    c.xs.free = [p]
                m = c.sm.take()
                for tp in range(2):
                    be, bo = c.ps.take(), c.ps.take()
                    for bk in (be, bo):
                        mm(bk.ap[:, :], identb, maskp[tp], *bk.free, start=True, stop=False)
                    for tq in range(2):
                        t = 2 * tp + tq
                        for i in range(4):
                            for g in range(4):
                                for e_, bk in enumerate((be, bo)):
                                    rows = slice(64 * e_, 64 * e_ + 64)
                                    o = 256 * tq + 64 * i
                                    last = tq == 1 and i == 3 and g == 3
                                    p = mm(bk.ap[32 * g:32 * g + 32, o:o + 64],
                                           c.qh[0].ap[rows, i, 128 * t + 32 * g:128 * t + 32 * g + 32],
                                           c.qh[1].ap[rows, i, 128 * t + 32 * g:128 * t + 32 * g + 64], qk16,
                                           start=False, stop=last, signal=last,
                                           tile_position=(64 * e_, 32 * g))
                    for e_, bk in enumerate((be, bo)):
                        mx = reduce(m.ap[:, 16 * tp:16 * tp + 16].rearrange("p (t e i) -> p t e i", t=2, e=2)[:, :, e_, :],
                                    bk.ap[:, :].rearrange("p (t i r) -> p t i r", t=2, i=4), ALU.max, p, *m.free)
                        bk.free = [mx]
                    yield
                c.qh[0].free, c.qh[1].free = [p], [p]
                yield
                bank = c.ps.take()
                for t in range(NT):
                    p = tr(bank.ap[0:8, 128 * t:128 * t + 128], m.ap[:, 8 * t:8 * t + 8], ident, mx, *bank.free,
                           signal=(t == NT - 1))
                m.free = [p]
                b3 = bank.ap[0:8, :].rearrange("p (t n) -> p t n", t=4)
                act(c.rhs.ap[96:104, :, 0:128], b3, ACT.Copy, p, *c.rhs.free, scale=-1.0)
                ng = act(c.rhs.ap[96:104, 0:3, 128:160], b3[:, 1:4, 0:32], ACT.Copy, scale=-1.0)
                bank.free = [ng]
                c.rhs.free = []
                yield

                def scores(t):
                    pt = c.pt.take()
                    for pair in range(2):
                        banks = (c.ps.take(), c.ps.take())
                        for e_, bk in enumerate(banks):
                            for y in range(2):
                                r = 4 * e_ + 2 * pair + y
                                mm(bk.ap[:, 160 * y:160 * y + 160], t_left[:, 128 * r:128 * r + 128],
                                   c.rhs.ap[:, t, :], ng, ready, *bk.free, start=(y == 0), stop=False)
                        for y in range(2):
                            for e_, bk in enumerate(banks):
                                rows = slice(64 * e_, 64 * e_ + 64)
                                i = 2 * pair + y
                                p = mm(bk.ap[:, 160 * y:160 * y + 160],
                                       c.qt[1].ap[rows, i, W + 128 * t:W + 128 * t + 128],
                                       c.qt[0].ap[rows, i, 128 * t:128 * t + 160], qk32,
                                       start=False, stop=(y == 1), signal=(y == 1))
                        for e_, bk in enumerate(banks):
                            ex = exp_split(c, bk, 320, pt, 160 * (4 * e_ + 2 * pair), p)
                        yield
                    pts[t] = (pt, ex)
                    if t == NT - 1:
                        c.qt[0].free, c.qt[1].free, c.rhs.free = [p], [p], [p]

                def values(t):
                    pt, ex = pts[t]
                    banks = (c.ps.take(), c.ps.take())
                    for e_, bk in enumerate(banks):
                        for i in range(4):
                            r = 4 * e_ + i
                            p = mm3(bk.ap[:, 65 * i:65 * i + 65],
                                    tuple(pt.ap[:, z, 160 * r:160 * r + 128] for z in range(2)),
                                    tuple(c.v.ap[:, z, t, 2 * i + e_, :] for z in range(2)), ex, v_done, *bk.free,
                                    start=(i == 0), stop=(i == 3), signal=(i == 3))
                    if t:
                        prev = pts[t - 1][0]
                        for e_, bk in enumerate(banks):
                            for i in range(4):
                                r = 4 * e_ + i
                                p = mm3(bk.ap[0:32, 65 * i:65 * i + 65],
                                        tuple(prev.ap[96:128, z, 160 * r + 128:160 * r + 160] for z in range(2)),
                                        tuple(c.v.ap[96:128, z, t - 1, 2 * i + e_, :] for z in range(2)),
                                        start=False, stop=(i == 3), signal=(i == 3), tile_position=(96, 0))
                        prev_place = pts[t - 1][0]
                        prev_place.free = [p]
                    if t == NT - 1:
                        pt.free = [p]
                        c.v.free = [p]
                    wo_ = c.wk.take()
                    for e_, bk in enumerate(banks):
                        rc = c.sm.take()
                        pv = bk.ap[:, 0:260].rearrange("p (a b) -> p a b", a=4)
                        d = recip(rc.ap[:, 0:4], pv[:, :, 64], p, *rc.free)
                        o = tt(DV, wo_.ap[:, :].rearrange("p (i e d) -> p i e d", i=4, e=2)[:, :, e_, :], pv[:, :, 0:64],
                               rc.ap[:, 0:4].unsqueeze(2).to_broadcast([128, 4, 64]), ALU.mult, d, *wo_.free)
                        rc.free = [o]
                        bk.free = [o]
                    return wo_, o

                pts, outs = {}, {}
                for t in range(NT + 2):
                    if t < NT:
                        yield from scores(t)
                    if 0 <= t - 1 < NT:
                        outs[t - 1] = values(t - 1)
                        yield
                    if t >= 2:
                        e = finish_heads(c, half, outs[t - 2][0], t - 2, outs[t - 2][1])
                        yield
                        if (t - 2) % 2:
                            last, done = project_out(c, half, (t - 2) // 2, e, c.wo_in)
                            yield
                        elif t == 2:
                            pass
            a = tt(DV, xb[0:64, b, 0:S], xb[0:64, b, 0:S], c.acc.ap[0:64, :], ALU.add, done, xt_, *x_read[b])
            a = tt(DV, xb[64:128, b, 1:S + 1], xb[64:128, b, 1:S + 1], c.acc.ap[64:128, :], ALU.add, done)
            c.x1 = a
            c.acc.free = [a]
            yield
            wx = c.wk.take()
            done, read = layernorm(c, xb[:, b, 0:S], wx.ap[:, :], c.x1, *wx.free)
            xn_kept[b] = SP.dma(s_xo[b], xnd[b], wx.ap[:, :], done)
            wx.free = [xn_kept[b]]
            x_ready[b], x_read[b] = c.x1, [read]
            yield

        def feed(c, b, li):
            us = []
            xin, t_in = xn_in.pop(b)
            for j in range(3):
                n = FP[j]
                ba, bg = c.ps.take(), c.ps.take()
                mm(ba.ap[0:n, :], w1r[:, 128 * j:128 * j + n], xin.ap, t_in, c.w1_in, *ba.free)
                p = mm(bg.ap[0:n, :], w1r[:, FF + 128 * j:FF + 128 * j + n], xin.ap, *bg.free, signal=True)
                g, u = c.wk.take(), c.wk.take()
                ge = act(g.ap[0:n, :], bg.ap[0:n, :], ACT.Gelu, p, c.b1_in, *g.free, bias=b1s[0:n, 3 + j:4 + j])
                ud = stt(u.ap[0:n, :], ba.ap[0:n, :], b1s[0:n, j:j + 1], g.ap[0:n, :], ALU.add, ALU.mult, ge, *u.free)
                bg.free, ba.free, g.free = [ge], [ud], [ud]
                us.append((u, ud))
                yield
            xin.free = [p]
            if b + 4 < NB:
                fetch(xin, b + 4)
            bank = c.ps.take()
            for j in range(3):
                n = FP[j]
                p = mm(bank.ap[:, :], w2r[0:n, j, :], us[j][0].ap[0:n, :], us[j][1], c.w2_in, *bank.free,
                       start=(j == 0), stop=(j == 2), signal=(j == 2))
                us[j][0].free = [p]
            us[0][0].free = us[1][0].free = us[2][0].free = [p]
            w2_read.append(p)
            b2 = t_vec[:, V_LAYER + 10 * li + 2:V_LAYER + 10 * li + 3]
            a = stt(xb[0:64, b, 0:S], bank.ap[0:64, :], b2[0:64, :], xb[0:64, b, 0:S], ALU.add, ALU.add, p,
                    x_ready[b], *x_read[b])
            a = stt(xb[64:128, b, 1:S + 1], bank.ap[64:128, :], b2[64:128, :], xb[64:128, b, 1:S + 1],
                    ALU.add, ALU.add, p)
            bank.free = [a]
            x_ready[b] = a
            x_read[b] = []
            yield

        def together(works, offset):
            live = [[(n * offset), n, (y for w in ws for y in w)] for n, ws in enumerate(works)]
            while live:
                live.sort(key=lambda x: (x[0], x[1]))
                before = work[0]
                try:
                    next(live[0][2])
                    live[0][0] += max(work[0] - before, 64)
                except StopIteration:
                    live.pop(0)

        def fetch(place, b):
            xn_in[b] = (place, SP.dma(s_xi[b], place.ap, xnd[b], xn_kept[b], *place.free))

        s_x1 = [slot(f"x1_{b}") for b in range(NB)]
        x1d = nc.dram_tensor("x1_keep", [NB, 128, S], F32).ap()
        kept = {}
        xnd = nc.dram_tensor("xn_keep", [NB, 128, S], F32).ap()
        s_xo = [slot(f"xo{b}") for b in range(NB)]
        s_xi = [slot(f"xi{b}") for b in range(NB)]
        xn_kept, xn_in = {}, {}
        for n, c in enumerate(C):
            c.n = n
            c.vt = 0
            c.obig = Place(c.qt[1].ap.rearrange("p a b -> p (a b)")[:, 544:1568].rearrange("p (a d) -> p a d", a=4))
        together([[causal(C[n], b) for b in range(n, NB, 2)] for n in range(2)], 8000)
        fold_read = [(PE.name, PE.count, PE.sem)]

        s_w1, s_w2, s_scl, s_tab, s_st = slot("w1"), slot("w2"), slot("scl"), slot("tab"), [slot("st0"), slot("st1")]
        wo_read, w2_read = [], []
        rot = None
        b1d = None
        for li in range(L):
            big_free = fold_read if li == 0 else qkv_read
            for n in range(6):
                st = wstage.take()
                t_st = SP.dma(s_st[n % 2], st.ap[:, :], wqkv[li, :, 512 * n:512 * n + 512], *st.free)
                hi = wsplit[:, 512 * n:512 * n + 512]
                a = act(hi, st.ap[:, :], ACT.Copy, t_st, *big_free, scale=WS)
                w_in = stt(wsplit[:, 3072 + 512 * n:3584 + 512 * n], st.ap[:, :], WS, hi, ALU.mult, ALU.subtract, a)
                st.free = [w_in]
            wo_in2 = SP.dma(s_wo, wout[:, :, :], wof[li].rearrange("(a p) c -> p a c", p=128), *big_free)
            scl_in = SP.dma(s_scl, t_scl[:, :, :].rearrange("p a b -> p (a b)"), scl[li], rot)
            for n in range(2):
                tab_in = SP.dma(s_tab, t_rots[:, n, :], tab[n], *big_free)
            w1_in = SP.dma(s_w1, w1r, w1[li], *w2_read, b1d, *(fold_read if li == 0 else []))
            for j in range(3):
                w2_in = SP.dma(s_w2, w2r[0:FP[j], j, :], w2[li, 128 * j:128 * j + FP[j], :], *w2_read)
            r1 = tt(GP, t_rot[0], t_rot[0], t_scl[:, :, :].unsqueeze(1).to_broadcast([128, NT, 2, DH]), ALU.mult,
                    scl_in, tab_in)
            rot = r1
            for e_ in range(2):
                half_ = t_rot[1][:, :, :, 32 * e_:32 * e_ + 32]
                rot = tt(GP, half_, half_,
                         t_scl[:, :, 32 * (1 - e_):32 * (1 - e_) + 32].unsqueeze(1).to_broadcast([128, NT, 2, 32]),
                         ALU.mult, rot)
            bank = C[0].ps.take()
            vl = V_LAYER + 10 * li
            for k in range(2):
                for j in range(3):
                    n = FP[j]
                    pb = mm(bank.ap[0:n, 3 * k + j:3 * k + j + 1], w1r[:, FF * k + 128 * j:FF * k + 128 * j + n],
                            t_vec[:, vl + 1:vl + 2], w1_in, *bank.free, start=(k == 0 and j == 0), stop=True,
                            signal=True)
            for k in range(2):
                tt(DV, b1s[:, 3 * k:3 * k + 2], bank.ap[:, 3 * k:3 * k + 2], t_vec[:, vl + 4 + 3 * k:vl + 6 + 3 * k],
                   ALU.add, pb, *w2_read)
                b1d = tt(DV, b1s[0:FP[2], 3 * k + 2:3 * k + 3], bank.ap[0:FP[2], 3 * k + 2:3 * k + 3],
                         t_vec[0:FP[2], vl + 6 + 3 * k:vl + 7 + 3 * k], ALU.add)
            bank.free = [b1d]
            w1s = ts(DV, w1r, w1r, t_vec[:, vl:vl + 1], None, ALU.mult, None, b1d)
            for c in C:
                c.w_in, c.wo_in, c.rot, c.w1_in, c.b1_in, c.w2_in = w_in, wo_in2, rot, w1s, b1d, w2_in
            wo_read.clear()
            tables("natural_log_exp_and_others")
            together([[local(C[n], b, li) for b in range(n, NB, 2)] for n in range(2)], 20000)
            tables("gelu_and_others")
            qkv_read = [(PE.name, PE.count, PE.sem), (GP.name, GP.count, GP.sem), (DV.name, DV.count, DV.sem)]
            w2_read.clear()
            for c in C:
                fetch(Place(c.acc.ap[:, :]), c.n)
                fetch(Place(c.xs.ap[:, :, :].rearrange("p a b -> p (a b)").bitcast(F32)), c.n + 2)
            together([[feed(C[n], b, li) for b in range(n, NB, 2)] for n in range(2)], 0)
            for c in C:
                c.acc.free, c.xs.free = [w2_read[-1]], [w2_read[-1]]
            b1d = w2_read[-1]

        s_out, s_x1r = slot("out"), [slot(f"x1r{b}") for b in range(NB)]
        fold_done = qkv_read
        for b in range(NB):
            y = C[b % 2].qt[b // 4].ap[:, b // 2 % 2, 0:S]
            back = SP.dma(s_x1r[b], y, x1d[b], kept[b], *fold_done)
            z = stt(y[0:64, :], xb[0:64, b, 0:S], t_mod[0:64, 5, b:b + 1], y[0:64, :], ALU.mult, ALU.add,
                    back, x_ready[b])
            z = stt(y[64:128, :], xb[64:128, b, 1:S + 1], t_mod[64:128, 5, b:b + 1], y[64:128, :],
                    ALU.mult, ALU.add)
            o = SP.dma(s_out, out[b], y, z)
        SP.wait(o)

        block = ctx.enter_context(nc.Block())

        @block.sync
        def _(e):
            SP.play(e)

        @block.tensor
        def _(e):
            PE.play(e)

        @block.scalar
        def _(e):
            AC.play(e)

        @block.vector
        def _(e):
            DV.play(e)

        @block.gpsimd
        def _(e):
            GP.play(e)


def kernel(**inputs):
    import concourse.bacc as _bacc
    from concourse.bass_utils import run_bass_kernel_spmd as _run

    a = {k: np.asarray(v) for k, v in inputs.items()}
    f = np.float32
    vecs = np.zeros((128, V_COLS), f)
    vecs[:, V_BO] = a["L0_attn_bo"]
    for li in range(L):
        o = V_LAYER + 10 * li
        vecs[:, o] = a["L0_ffn_ln_g"][li]
        vecs[:, o + 1] = a["L0_ffn_ln_b"][li]
        vecs[:, o + 2] = a["L0_ffn_b2"][li]
        for k in range(2):
            for j in range(3):
                vecs[0:FP[j], o + 4 + 3 * k + j] = a["L0_ffn_b1"][li][FF * k + 128 * j:FF * k + 128 * j + FP[j]]
    scl = np.concatenate([a["L0_ffn_q_scale"], a["L0_ffn_k_scale"]], 1)
    arrays = {
        "xt": a["L0_attn_x"].transpose(0, 2, 1),
        "wqt": a["L0_attn_Wq"].T, "wkt": a["L0_attn_Wk"].T, "wv": a["L0_attn_Wv"], "wo": a["L0_attn_Wo"],
        "wqkv": a["L0_ffn_Wqkv"], "wof": a["L0_ffn_Wo"], "w1": a["L0_ffn_W1"], "w2": a["L0_ffn_W2"],
        "vecs": vecs, "scl": np.broadcast_to(scl[:, None, :], (L, 128, 2 * DH)), "ct": a["L0_c"].T, "wmod": a["L0_wmod"],
    }
    arrays.update(constants())
    arrays = {k: np.ascontiguousarray(v) for k, v in arrays.items()}
    nc = _bacc.Bacc("TRN2", target_bir_lowering=False, num_devices=1)
    args = {k: nc.dram_tensor(k, v.shape, mybir.dt.from_np(v.dtype), kind="ExternalInput").ap() for k, v in arrays.items()}
    args["out"] = nc.dram_tensor("out", (NB, 128, S), F32, kind="ExternalOutput").ap()
    program(nc, **args)
    r = _run(nc, [arrays], core_ids=[0])
    return r.results[0]["out"].transpose(0, 2, 1)
```

```python
from contextlib import ExitStack

import numpy as np

import concourse.bass as bass
from concourse import mybir

F32 = mybir.dt.float32
BF16 = mybir.dt.bfloat16
F16 = mybir.dt.float16
ALU = mybir.AluOpType
ACT = mybir.ActivationFunctionType
AXX = mybir.AxisListType.X

NB = 8
S = 512
D = 128
NH = 16
DH = 64
L = 6
W = 32
NT = S // 128
FF = 341
FP = [128, 128, FF - 256]
NEG = -1e30
LN2 = 0.6931471805599453
WK = (6, 4)
WU = (4, 4)
WS = 64.0
PSTEPS = 21
CSTEPS = 17
AHEAD = 1.0
V_BO, V_LAYER, V_B1 = 0, 1, 5
V_COLS = 1 + L * 10


class Queue:

    def __init__(self, name, sem):
        self.name, self.sem, self.count, self.items, self.waited = name, sem, 0, [], {}

    def wait(self, *tokens):
        need = {}
        for t in tokens:
            if t is not None and t[1] > need.get(t[0], (None, 0))[1]:
                need[t[0]] = t
        for key, t in need.items():
            if self.waited.get(key, 0) < t[1]:
                self.waited[key] = t[1]
                self.items.append(("wait", t[2], t[1]))

    def do(self, fn, *tokens, signal=True):
        self.wait(*tokens)
        if signal:
            self.count += 1
            self.items.append(("do", fn, self.sem, 1))
            return (self.name, self.count, self.sem)
        self.items.append(("do", fn, None, 0))
        return None

    def dma(self, slot, out, in_, *tokens):
        self.wait(*tokens)
        slot.count += 16
        self.items.append(("do", lambda e: e.dma_start(out, in_), slot.sem, 16))
        return (slot.name, slot.count, slot.sem)

    def play(self, eng):
        for it in self.items:
            if it[0] == "wait":
                eng.wait_ge(it[1], it[2])
            else:
                ins = it[1](eng)
                if it[2] is not None:
                    ins.then_inc(it[2], it[3])


class Slot:

    def __init__(self, name, sem):
        self.name, self.sem, self.count = name, sem, 0


class Place:

    def __init__(self, ap):
        self.ap, self.free = ap, []


class Ring:
    def __init__(self, places):
        self.places, self.at = places, 0

    def take(self):
        p = self.places[self.at % len(self.places)]
        self.at += 1
        return p


def constants():
    f = np.float32
    pos = np.arange(S)
    half = np.arange(0, DH, 2, dtype=f)
    inv = (f(1.0) / np.power(f(10000.0), half / f(DH))).astype(f)
    freqs = (pos.astype(f)[:, None] * inv[None, :]).astype(f).astype(np.float64)
    base = ((half + f(0.4 * DH)) / f(1.4 * DH)).astype(f).astype(np.float64)
    scale = base[None, :] ** ((pos - S // 2) / (W // 2))[:, None]
    cos, sin = np.cos(freqs), np.sin(freqs)
    rows = []
    for s in (8.0 * scale, 1.0 / scale):
        rows.append((np.concatenate([cos * s, cos * s], -1), np.concatenate([-sin * s, sin * s], -1)))
    tab = np.zeros((2, 128, NT, 2, DH), f)
    for qk in range(2):
        for cs in range(2):
            tab[cs, :, :, qk, :] = rows[qk][cs].reshape(NT, 128, DH).transpose(1, 0, 2)
    p = np.arange(128)[:, None]
    r = np.arange(64)[None, :]
    pw = p % W
    ok = np.where(r < W, pw <= r, (r - W) <= pw)
    first = ok & ~((p < W) & (r < W))
    mp = np.where(ok, 0.0, NEG)
    mp0 = np.where(first, 0.0, NEG)
    maskp = np.stack([np.concatenate([np.tile(mp0, (1, 4)), np.tile(mp, (1, 4))], 1), np.tile(mp, (1, 8))], 1)
    left = np.zeros((104, 8, 128), f)
    right = np.zeros((104, 160), f)
    key, qry = np.arange(128), np.arange(160)
    left[32 * ((key // W) % 2) + key % W, :, key] = 1.0
    left[64 + key // W, :, key] = 1.0
    for r in range(8):
        left[96 + r, r, :] = 1.0
    for r in range(64):
        same = (qry // W) % 2 == r // 32
        right[r] = np.where(np.where(same, r % 32 > qry % W, r % 32 < qry % W), NEG, 0.0)
    for w in range(4):
        right[64 + w] = np.where((qry // W - w == 0) | (qry // W - w == 1), 0.0, NEG)
    q = np.arange(128)[:, None]
    k = np.arange(128)[None, :]
    maskaq = np.where(k <= q, 0.0, NEG)
    maskak = np.where(k >= q, 0.0, NEG)
    masks = np.concatenate([maskp.reshape(128, 1024), maskaq, maskak, np.eye(128)], 1).astype(f)
    mats = np.concatenate([np.eye(128), np.eye(128) - 1.0 / 128, np.full((128, 128), 1.0 / 128)], 1).astype(f)
    return {"tab": tab.reshape(2, 128, NT * 2 * DH), "masks": masks, "left": left.reshape(104, 1024), "right": right, "mats": mats}


def program(nc, xt, wqt, wkt, wv, wo, wqkv, wof, w1, w2, vecs, scl, ct, wmod, tab, masks, left, right, mats, out):
    ctx = ExitStack()
    with ctx:
        def sb(name, shape, dt=F32):
            return ctx.enter_context(nc.sbuf_tensor(name, shape, dt))

        def sem(name):
            return ctx.enter_context(nc.semaphore(name))

        PE = Queue("pe", sem("s_pe"))
        AC = Queue("act", sem("s_act"))
        DV = Queue("dve", sem("s_dve"))
        GP = Queue("pool", sem("s_pool"))
        SP = Queue("sync", None)

        def slot(name):
            return Slot(name, sem("s_" + name))

        t_mats = sb("t_mats", [128, 384])
        ident, center, mean = t_mats[:, 0:128], t_mats[:, 128:256], t_mats[:, 256:384]
        t_masks = sb("t_masks", [128, 1024 + 384], BF16)
        maskp = [t_masks[:, 512 * n:512 * n + 512] for n in range(2)]
        maskaq, maskak, identb = (t_masks[:, 1024 + 128 * n:1152 + 128 * n] for n in range(3))
        t_left = sb("t_left", [104, 8 * 128], BF16)
        t_rots = sb("t_rots", [128, 2, NT * 2 * DH])
        t_rot = [t_rots[:, n, :].rearrange("p (t k d) -> p t k d", t=NT, k=2) for n in range(2)]
        t_scl = sb("t_scl", [128, 2, DH])
        t_vec = sb("t_vec", [128, V_COLS])
        t_mod = sb("t_mod", [128, 6, NB])
        t_ct = sb("t_ct", [128, 3, NB])
        xb = sb("xb", [128, NB, S + 1])
        wbig = sb("wbig", [128, 3 * 1024])
        wsplit = wbig[:, :].bitcast(F16)
        wstage = Ring([Place(sb(f"wstage{i}", [128, 512])) for i in range(2)])
        wout = sb("wout", [128, 8, 128])
        w12 = sb("w12", [128, 2 * FF + 3 * 128])
        w1r = w12[:, 0:2 * FF]
        w2r = w12[:, 2 * FF:2 * FF + 384].rearrange("p (a b) -> p a b", a=3)
        b1s = sb("b1s", [128, 6])

        class Ctx:
            pass

        C = []
        for n in range(2):
            c = Ctx()
            c.qt = [Place(sb(f"qt{n}{x}", [128, 4, W + S])) for x in "qk"]
            c.qh = [Place(sb(f"qh{n}{x}", [128, 4, W + S], BF16)) for x in "qk"]
            c.v = Place(sb(f"v{n}", [128, 2, NT, 8, 65], F16))
            c.pt = Ring([Place(sb(f"pt{n}{i}", [128, 2, 8 * 160], F16)) for i in range(3)])
            c.wk = Ring([Place(sb(f"wk{n}{i}", [128, 512])) for i in range(WK[n])])
            c.wu = Ring([Place(sb(f"wu{n}{i}", [128, 512])) for i in range(WU[n])])
            c.ot = Place(sb(f"ot{n}", [128, 4, 256]))
            c.acc = Place(sb(f"acc{n}", [128, S]))
            c.xs = Place(sb(f"xs{n}", [128, 2, S], F16))
            c.rhs = Place(sb(f"rhs{n}", [104, NT, 160], BF16))
            c.sm = Ring([Place(sb(f"sm{n}{i}", [128, 32])) for i in range(8)])
            c.ps = Ring([Place(ctx.enter_context(nc.psum_tensor(f"ps{n}{i}", [128, 512], F32))) for i in range(4)])
            C.append(c)

        work = [0.0]

        def mm(o, l, r, *tokens, start=True, stop=True, signal=False, **kw):
            n = r.shape[-1] if len(r.shape) == 2 else int(np.prod(r.shape[1:]))
            work[0] += max(256, 4 * n) if l.dtype == F32 else max(64, n)
            return PE.do(lambda e: e.matmul(o, l, r, start=start, stop=stop, skip_group_check=True, **kw),
                         *tokens, signal=signal)

        def mm3(o, l, r, *tokens, start=True, stop=True, signal=False, **kw):
            mm(o, l[0], r[1], *tokens, start=start, stop=False, **kw)
            mm(o, l[1], r[0], start=False, stop=False, **kw)
            return mm(o, l[0], r[0], start=False, stop=stop, signal=signal, **kw)

        def tr(o, i, idn, *tokens, signal=False):
            work[0] += 128
            return PE.do(lambda e: e.transpose(o, i, idn), *tokens, signal=signal)

        def act(o, i, f, *tokens, **kw):
            return AC.do(lambda e: e.activation(o, i, f, **kw), *tokens)

        def tt(q, o, a, b, op, *tokens):
            return q.do(lambda e: e.tensor_tensor(o, a, b, op), *tokens)

        def ts(q, o, a, s1, s2, o0, o1, *tokens):
            if o1 is None:
                return q.do(lambda e: e.tensor_scalar(o, a, s1, None, o0), *tokens)
            return q.do(lambda e: e.tensor_scalar(o, a, s1, s2, o0, o1), *tokens)

        def copy(q, o, i, *tokens):
            return q.do(lambda e: e.tensor_copy(o, i), *tokens)

        def reduce(o, i, op, *tokens):
            return DV.do(lambda e: e.tensor_reduce(o, i, AXX, op), *tokens)

        def recip(o, i, *tokens):
            return DV.do(lambda e: e.reciprocal(o, i), *tokens)

        def fill(o, value, *tokens):
            return DV.do(lambda e: e.memset(o, value), *tokens)

        def stt(o, a, s, b, o0, o1, *tokens):
            return DV.do(lambda e: e.scalar_tensor_tensor(out=o, in0=a, scalar=s, in1=b, op0=o0, op1=o1), *tokens)

        s_c = slot("const")
        st_masks = C[0].qt[0].ap.rearrange("p a b -> p (a b)")[:, 0:1408]
        st_left = C[1].qt[0].ap.rearrange("p a b -> p (a b)")[0:104, 0:1024]
        st_right = C[1].qt[0].ap.rearrange("p a b -> p (a b)")[0:104, 1024:1184]
        for o, i in ((t_mats[:, :], mats), (st_masks, masks), (st_left, left), (st_right, right),
                     (t_vec[:, :], vecs), (t_ct[:, 0, :], ct)):
            const_in = SP.dma(s_c, o, i)
        s_x = slot("x")
        for b in range(NB):
            x_in = SP.dma(s_x, xb[:, b, 0:S], xt[b])
        s_wa = slot("wa")
        wqk_in = SP.dma(s_wa, wbig[:, 0:1024].rearrange("p (a c) -> p a c", a=8), wqt.rearrange("(a p) c -> p a c", p=128))
        wqk_in = SP.dma(s_wa, wbig[:, 1024:2048].rearrange("p (a c) -> p a c", a=8), wkt.rearrange("(a p) c -> p a c", p=128))
        wqk_in = wv_in = SP.dma(s_wa, wbig[:, 2048:3072], wv)
        s_wo = slot("wo")
        wo_in = SP.dma(s_wo, wout[:, :, :], wo.rearrange("(a p) c -> p a c", p=128))
        s_wm = slot("wm")
        t_wmod = C[0].pt.places[0].ap.rearrange("p a b -> p (a b)").bitcast(F32)[:, 0:768]
        wm_in = SP.dma(s_wm, t_wmod, wmod)

        pads = [copy(DV, t_masks[:, :], st_masks, const_in), copy(DV, t_left[:, :], st_left)]
        for c in C:
            for t in range(NT):
                pads.append(copy(DV, c.rhs.ap[:, t, :], st_right))
        t_eps = sb("t_eps", [128, 2])
        pads.append(fill(t_eps[:, 0:1], 1e-5, *pads))
        pads.append(fill(t_eps[:, 1:2], 10.0 * LN2))
        for c in C:
            for k in range(2):
                for t in (c.qt[k].ap, c.qh[k].ap):
                    pads.append(fill(t[:, :, S:S + W] if k == 0 else t[:, :, 0:W], 0.0, pads[-1]))
            pads.append(fill(c.v.ap[:, 0, :, :, 64:65], 1.0))
            pads.append(fill(c.v.ap[:, 1, :, :, 64:65], 0.0))
        ready = pads[-1]

        def tables(name):
            AC.do(lambda e: e.preload_act_table_set(name), signal=False)

        tables("natural_log_exp_and_others")

        ex = act(t_ct[:, 1, :], t_ct[:, 0, :], ACT.Exp, const_in, ready, scale=-1.0)
        a1 = ts(DV, t_ct[:, 1, :], t_ct[:, 1, :], 1.0, None, ALU.add, None, ex)
        a1 = recip(t_ct[:, 2, :], t_ct[:, 1, :], a1)
        silu = tt(DV, t_ct[:, 1, :], t_ct[:, 0, :], t_ct[:, 2, :], ALU.mult, a1)
        bank = C[0].ps.take()
        for j in range(6):
            pm = mm(bank.ap[:, 8 * j:8 * j + 8], t_wmod[:, 128 * j:128 * j + 128], t_ct[:, 1, :],
                    silu, wm_in, start=(j == 0), stop=(j == 5), signal=True)
        mod = copy(DV, t_mod[:, :, :].rearrange("p a b -> p (a b)"), bank.ap[:, 0:48], pm)
        bank.free = [mod]
        for j in (1, 4):
            mod = ts(DV, t_mod[:, j, :], t_mod[:, j, :], 1.0, None, ALU.add, None, mod)
        for j in (2, 5):
            g = t_mod[:, j, :]
            m1 = ts(DV, t_ct[:, 0, :], g, 0.0, None, ALU.is_ge, None, mod)
            m1 = ts(DV, t_ct[:, 0, :], t_ct[:, 0, :], 2.0, -1.0, ALU.mult, ALU.add, m1)
            m2 = ts(DV, t_ct[:, 2, :], g, -1.0, None, ALU.mult, None, m1)
            m2 = tt(DV, t_ct[:, 2, :], t_ct[:, 2, :], g, ALU.max, m2)
            m2 = ts(DV, t_ct[:, 2, :], t_ct[:, 2, :], 0.25, None, ALU.max, None, m2)
            mod = tt(DV, g, t_ct[:, 0, :], t_ct[:, 2, :], ALU.mult, m2)
        mods = mod
        C[0].pt.places[0].free = [pm]

        afold = [t_rots[:, :, :].rearrange("p a b -> p (a b)"), w12[:, 0:1024]]
        fold = []
        for g in range(4):
            bank_e, bank_o = C[g % 2].ps.take(), C[g % 2].ps.take()
            for r in range(4):
                h = 4 * g + r
                bk = (bank_e, bank_o)[h % 2]
                rows = slice(64 * (h % 2), 64 * (h % 2) + 64)
                pm = mm(bk.ap[:, 128 * (r // 2):128 * (r // 2) + 128],
                        wbig[rows, 128 * (h // 2):128 * (h // 2) + 128],
                        wbig[rows, 1024 + 128 * (h // 2):1152 + 128 * (h // 2)], wqk_in, *bk.free,
                        signal=True)
            dst = afold[g // 2][:, 512 * (g % 2):512 * (g % 2) + 512].rearrange("p (a e c) -> p a e c", a=2, e=2)
            for e_, bk in enumerate((bank_e, bank_o)):
                f = act(dst[:, :, e_, :], bk.ap[:, 0:256].rearrange("p (a c) -> p a c", a=2), ACT.Copy, pm, scale=0.125)
                bk.free = [f]
            fold.append(f)
        fold = fold[-1]

        x_ready = {b: x_in for b in range(NB)}
        x_read = {b: [] for b in range(NB)}

        def rsqrt_start(src, dst, tmp, shift, *tokens):
            sc, bi = (2.0 ** 20, t_eps[:, 1:2]) if shift else (1.0, 0.0)
            a = act(tmp, src, ACT.Ln, *tokens, scale=sc)
            return act(dst, tmp, ACT.Exp, a, scale=-0.5, bias=bi)

        def rsqrt_end(src, dst, tmp, a):
            d = tt(DV, tmp, dst, dst, ALU.mult, a)
            d = tt(DV, tmp, tmp, src, ALU.mult, d)
            d = ts(DV, tmp, tmp, -0.5, 1.5, ALU.mult, ALU.add, d)
            return tt(DV, dst, dst, tmp, ALU.mult, d)

        def layernorm_start(c, src, t_src):
            pc, wq, wc = c.ps.take(), c.wu.take(), c.wu.take()
            ctr = mm(pc.ap[:, :], center, src, t_src, *pc.free, signal=True)
            sq = act(wq.ap[:, :], pc.ap[:, :], ACT.Square, ctr, *wq.free)
            mid = act(wc.ap[:, :], pc.ap[:, :], ACT.Copy, *wc.free)
            pc.free = [mid]
            return wq, wc, sq, mid, ctr

        def layernorm_mid(c, started):
            wq, wc, sq, mid, ctr = started
            pv, wr, wt = c.ps.take(), c.wk.take(), c.wk.take()
            var = mm(pv.ap[:, :], mean, wq.ap[:, :], sq, *pv.free, signal=True)
            v = ts(DV, wr.ap[:, :], pv.ap[:, :], 1e-5, None, ALU.add, None, var, *wr.free)
            pv.free = [v]
            a = rsqrt_start(wr.ap[:, :], wq.ap[:, :], wt.ap[:, :], False, v, *wt.free)
            return wq, wc, wr, wt, mid, ctr, a

        def layernorm_end(c, started, dst=None, *dst_free):
            wq, wc, wr, wt, mid, ctr, a = started
            r = rsqrt_end(wr.ap[:, :], wq.ap[:, :], wt.ap[:, :], a)
            done = tt(DV, wc.ap[:, :] if dst is None else dst, wc.ap[:, :], wq.ap[:, :], ALU.mult, r, mid, *dst_free)
            wc.free, wq.free, wr.free, wt.free = [done], [done], [done], [done]
            return done, ctr

        def layernorm(c, src, dst, t_src, *dst_free):
            return layernorm_end(c, layernorm_mid(c, layernorm_start(c, src, t_src)), dst, *dst_free)

        def finish_heads(c, ot, o_place, t, o_done):
            bank = c.ps.take()
            for i in range(4):
                p = tr(bank.ap[:, 128 * i:128 * i + 128], o_place.ap[:, 128 * i:128 * i + 128], ident,
                       o_done, *bank.free, signal=(i == 3))
            o_place.free = [p]
            e = act(ot.ap[:, :, 128 * (t % 2):128 * (t % 2) + 128], bank.ap[:, :].rearrange("p (a b) -> p a b", a=4),
                    ACT.Copy, p, *ot.free)
            bank.free = [e]
            return e

        def project_out(c, ot, acc, half, tp, ot_done, w_in):
            bank = c.ps.take()
            for i in range(4):
                p = mm(bank.ap[:, 0:256], wout[:, 4 * half + i, :], ot.ap[:, i, :], ot_done, w_in, *bank.free,
                       start=(i == 0), stop=(i == 3), signal=(i == 3))
            ot.free = [p]
            a = acc.ap[:, 256 * tp:256 * tp + 256]
            if half == 0:
                done = act(a, bank.ap[:, 0:256], ACT.Copy, p, *acc.free)
                acc.half = done
            else:
                done = tt(DV, a, bank.ap[:, 0:256], a, ALU.add, p, acc.half)
            bank.free = [done]
            return done

        def v_chunk(c, place, t, l, r, scale, *tokens):
            bank = c.ps.take()
            if isinstance(l, tuple):
                p = mm3(bank.ap[:, :], l, r, *tokens, *bank.free, signal=True)
            else:
                p = mm(bank.ap[:, :], l, r, *tokens, *bank.free, signal=True)
            b3 = bank.ap[:, :].rearrange("p (h d) -> p h d", h=8)
            v = act(place.ap[:, 0, t, :, 0:64], b3, ACT.Copy, p, ready, *place.free, scale=scale)
            v = stt(place.ap[:, 1, t, :, 0:64], b3, scale, place.ap[:, 0, t, :, 0:64], ALU.mult, ALU.subtract, v)
            bank.free = [v]
            return p, v

        def exp_split(c, banks, n, pt, offs, p, hi_q=DV, lo_q=GP):
            made = []
            for bank in banks:
                w_ = c.wk.take()
                ex = act(w_.ap[:, 0:n], bank.ap[:, 0:n], ACT.Exp, p, *w_.free)
                bank.free = [ex]
                made.append((w_, ex))
            for (w_, ex), off in zip(made, offs):
                if hi_q is AC:
                    hi = act(pt.ap[:, 0, off:off + n], w_.ap[:, 0:n], ACT.Copy, ex, *pt.free)
                else:
                    hi = copy(DV, pt.ap[:, 0, off:off + n], w_.ap[:, 0:n], ex, *pt.free)
                lo = tt(lo_q, pt.ap[:, 1, off:off + n], w_.ap[:, 0:n], pt.ap[:, 0, off:off + n], ALU.subtract, hi)
                w_.free = [lo]
            return lo

        def causal(c, b):
            ht, hh = c.qt[1].ap[:, 0, 0:S], c.qh[1].ap[:, 0, 0:S]
            ngm_a = c.rhs.ap[96:100, :, :].rearrange("p a b -> p (a b)")[:, 0:S]
            sel_a = t_left[96:100, :]
            done, read = layernorm(c, xb[:, b, 0:S], ht, x_ready[b], *c.qt[1].free, *c.qh[1].free)
            hdone = ts(DV, ht, ht, t_mod[:, 1, b:b + 1], t_mod[:, 0, b:b + 1], ALU.mult, ALU.add, done, mods)
            hcast = copy(DV, hh, ht, hdone)
            yield
            last = None
            for half in range(2):
                for t in range(NT):
                    p, v_done = v_chunk(c, c.v, t, ht[:, 128 * t:128 * t + 128], wbig[:, 2048 + 512 * half:2560 + 512 * half],
                                        1.0, hdone, wv_in)
                    yield
                c.v.free = []
                o_half = c.obig
                for g in range(2):
                    yt, yh = c.qt[0].ap, c.qh[0].ap
                    for r in range(4):
                        h = 8 * half + 4 * g + r
                        bank = c.ps.take()
                        p = mm(bank.ap[:, :], afold[half][:, 128 * (h % 8):128 * (h % 8) + 128], ht, hdone, fold, *bank.free, signal=True)
                        y1 = act(yt[:, r, 0:S], bank.ap[:, :], ACT.Copy, p, *c.qt[0].free)
                        y2 = copy(DV, yh[:, r, 0:S], yt[:, r, 0:S], y1, *c.qh[0].free)
                        bank.free = [y1]
                        yield
                    c.qt[0].free, c.qh[0].free = [], []
                    yield
                    m = c.sm.take()
                    for i in range(NT):
                        for r in range(4):
                            bank = c.ps.take()
                            n = 128 * (i + 1)
                            mm(bank.ap[:, 0:n], yh[:, r, 128 * i:128 * i + 128], hh[:, 0:n], y2, hcast, *bank.free,
                               start=True, stop=False)
                            p = mm(bank.ap[:, n - 128:n], identb, maskaq, start=False, stop=True, signal=True)
                            mx = reduce(m.ap[:, 4 * i + r:4 * i + r + 1], bank.ap[:, 0:n], ALU.max, p, *m.free)
                            bank.free = [mx]
                        yield
                    c.qh[0].free = [p]
                    bank = c.ps.take()
                    for i in range(NT):
                        p = tr(bank.ap[0:4, 128 * i:128 * i + 128], m.ap[:, 4 * i:4 * i + 4], ident, mx, *bank.free,
                               signal=(i == NT - 1))
                    m.free = [p]
                    ng = act(ngm_a[:, :], bank.ap[0:4, :], ACT.Copy, p, *c.rhs.free, scale=-1.0)
                    bank.free = [ng]
                    yield
                    offs = [0, 512, 896, 1152]
                    pts = {}

                    def scores(r):
                        pt = pts[r] = c.pt.take()
                        for j in range(NT):
                            n = S - 128 * j
                            bank = c.ps.take()
                            mm(bank.ap[:, 0:n], ht[:, 128 * j:128 * j + 128], yt[:, r, 128 * j:S], y1, hdone,
                               *bank.free, start=True, stop=False)
                            mm(bank.ap[:, 0:n], sel_a[:, 128 * r:128 * r + 128], ngm_a[:, 128 * j:S], ng,
                               start=False, stop=False)
                            p = mm(bank.ap[:, 0:128], identb, maskak, start=False, stop=True, signal=True)
                            ex = exp_split(c, [bank], n, pt, [offs[j]], p)
                            yield
                        pts[r] = (pt, ex)

                    def values(r):
                        h8 = 4 * g + r
                        pt, ex = pts[r]
                        bank = c.ps.take()
                        first = True
                        for i in range(NT):
                            for j in range(i + 1):
                                at = offs[j] + 128 * (i - j)
                                p = mm3(bank.ap[:, 65 * i:65 * i + 65],
                                        (pt.ap[:, 0, at:at + 128], pt.ap[:, 1, at:at + 128]),
                                        (c.v.ap[:, 0, j, h8, :], c.v.ap[:, 1, j, h8, :]),
                                        ex, v_done, *bank.free, start=first, stop=(i == NT - 1 and j == i),
                                        signal=(i == NT - 1 and j == i))
                                first = False
                        pt.free = [p]
                        rc = c.sm.take()
                        pv = bank.ap[:, 0:260].rearrange("p (a b) -> p a b", a=4)
                        d = recip(rc.ap[:, 0:4], pv[:, :, 64], p, *rc.free)
                        o = tt(DV, o_half.ap[:, :, 64 * r:64 * r + 64], pv[:, :, 0:64],
                               rc.ap[:, 0:4].unsqueeze(2).to_broadcast([128, 4, 64]), ALU.mult, d, *o_half.free, mods)
                        rc.free = [o]
                        bank.free = [o]
                        return p, o

                    for r in range(5):
                        if r < 4:
                            yield from scores(r)
                        if r > 0:
                            p, o = values(r - 1)
                            yield
                    c.qt[0].free = [p]
                    c.rhs.free = [p]
                    c.v.free = [p]
                    for tp in range(2):
                        bank = c.ps.take()
                        for y in range(4):
                            t, i = 2 * tp + y // 2, y % 2
                            p = tr(bank.ap[:, 128 * y:128 * y + 128], o_half.ap[:, t, 128 * i:128 * i + 128], ident, o,
                                   *bank.free, signal=(y == 3))
                        ot = c.ot.ap[:, 2 * tp:2 * tp + 2, :].rearrange("p a n -> p (a n)")
                        e = act(ot.rearrange("p (i t n) -> p t i n", i=2, t=2),
                                bank.ap[:, :].rearrange("p (t i n) -> p t i n", t=2, i=2), ACT.Copy, p, *c.ot.free)
                        bank.free = [e]
                    o_half.free = [p]
                    c.ot.free = []
                    yield
                    for tp in range(2):
                        bank = c.ps.take()
                        for i in range(2):
                            p = mm(bank.ap[:, 0:256], wout[:, 4 * half + 2 * g + i, :], c.ot.ap[:, 2 * tp + i, :],
                                   e, wo_in, *bank.free, start=(i == 0), stop=(i == 1), signal=(i == 1))
                        a = c.acc.ap[:, 256 * tp:256 * tp + 256]
                        if half == 0 and g == 0:
                            done = act(a, bank.ap[:, 0:256], ACT.Copy, p, *c.acc.free)
                            first_acc = done
                        else:
                            done = tt(DV, a, bank.ap[:, 0:256], a, ALU.add, p, first_acc, last)
                        bank.free = [done]
                    last = done
                    c.ot.free = [p]
                    yield
            z = ts(DV, c.acc.ap[:, :], c.acc.ap[:, :], t_vec[:, V_BO:V_BO + 1], t_mod[:, 2, b:b + 1],
                   ALU.add, ALU.mult, last)
            c.x1 = tt(DV, xb[:, b, 0:S], xb[:, b, 0:S], c.acc.ap[:, :], ALU.add, z, read)
            c.acc.free = [c.x1]
            last = p
            c.qt[1].free, c.qh[1].free = [last], [last]
            x1 = c.x1
            wp = c.wk.take()
            keep = SP.dma(s_x1[b], x1d[b], xb[:, b, 0:S], x1)
            done, read = layernorm(c, xb[:, b, 0:S], wp.ap[:, :], x1, *wp.free)
            z = fill(xb[64:128, b, 0:1], 0.0, read, keep)
            a = ts(DV, xb[0:64, b, 0:S], wp.ap[0:64, :], t_mod[0:64, 4, b:b + 1], t_mod[0:64, 3, b:b + 1],
                   ALU.mult, ALU.add, done, keep)
            a2 = ts(DV, xb[64:128, b, 1:S + 1], wp.ap[64:128, :], t_mod[64:128, 4, b:b + 1],
                    t_mod[64:128, 3, b:b + 1], ALU.mult, ALU.add, done, z)
            wp.free = [a2]
            x_ready[b] = a2
            kept[b] = keep
            yield

        def split_x(b):
            to, src = C[b % 2].xs, xb[:, b, 0:S]
            xh = copy(DV, to.ap[:, 0, :], src, x_ready[b], *to.free)
            to.done = tt(DV, to.ap[:, 1, :], src, to.ap[:, 0, :], ALU.subtract, xh)

        def produce(u):
            c, (b, half), to = C[0], divmod(u, 2), C[u % 2]
            x_split = C[b % 2].xs
            if u == 0:
                split_x(0)
            if half and b + 1 < NB:
                split_x(b + 1)
            xs = x_split.done

            def x_of(t):
                return tuple(x_split.ap[:, z, 128 * t:128 * t + 128] for z in range(2))

            def w_of(col):
                return tuple(wsplit[:, 3072 * z + col:3072 * z + col + 512] for z in range(2))

            q3 = lambda a: a.rearrange("p (h d) -> p h d", h=8)
            q4 = lambda a: a.rearrange("p (h e d) -> p h e d", h=8, e=2)

            def project(t):
                s1, s2, s3 = c.sm.take(), c.sm.take(), c.sm.take()
                banks, sqs = (c.ps.take(), c.ps.take()), (c.wk.take(), c.wk.take())
                for k in range(2):
                    p = mm3(banks[k].ap[:, :], x_of(t), w_of(1024 * k + 512 * half), xs, c.w_in, *banks[k].free,
                            signal=True)
                    sq = act(sqs[k].ap[:, :], banks[k].ap[:, :], ACT.Square, p, *sqs[k].free)
                    ss = reduce(s1.ap[:, 8 * k:8 * k + 8], q3(sqs[k].ap[:, :]), ALU.add, sq, *s1.free)
                ss = ts(DV, s1.ap[:, 0:16], s1.ap[:, 0:16], WS * WS * 1e-24, None, ALU.max, None, ss)
                return banks, sqs, (s1, s2, s3), ss

            def inverse_norm(sms, ss):
                s1, s2, s3 = sms
                return rsqrt_start(s1.ap[:, 0:16], s2.ap[:, 0:16], s3.ap[:, 0:16], True, ss, *s2.free, *s3.free)

            def rotate(t, banks, sqs, sms, rn):
                s1, s2, s3 = sms
                rn = rsqrt_end(s1.ap[:, 0:16], s2.ap[:, 0:16], s3.ap[:, 0:16], rn)
                made = []
                for k in range(2):
                    wn, wu, ww, bank = c.wk.take(), c.wu.take(), sqs[k], banks[k]
                    n = tt(DV, q3(wn.ap[:, :]), q3(bank.ap[:, :]),
                           s2.ap[:, 8 * k:8 * k + 8].unsqueeze(2).to_broadcast([128, 8, 64]), ALU.mult, rn, *wn.free)
                    bank.free = [n]
                    u = tt(DV, q3(wu.ap[:, :]), q3(wn.ap[:, :]),
                           t_rot[0][:, t, k, :].unsqueeze(1).to_broadcast([128, 8, 64]), ALU.mult, n, c.rot, *wu.free)
                    v = n
                    for e_ in range(2):
                        v = tt(GP, q4(ww.ap[:, :])[:, :, e_, :], q4(wn.ap[:, :])[:, :, 1 - e_, :],
                               t_rot[1][:, t, k, 32 * e_:32 * e_ + 32].unsqueeze(1).to_broadcast([128, 8, 32]),
                               ALU.mult, v, n, c.rot)
                    w_ = tt(GP, wu.ap[:, :], wu.ap[:, :], ww.ap[:, :], ALU.add, v, u)
                    wn.free, ww.free = [u, v], [w_]
                    made.append((wu, w_))
                for s_ in sms:
                    s_.free = [n]
                return made

            def turn(k, t, wu, w_):
                bank = c.ps.take()
                for i in range(4):
                    p = tr(bank.ap[:, 128 * i:128 * i + 128], wu.ap[:, 128 * i:128 * i + 128], ident, w_,
                           *bank.free, signal=(i == 3))
                wu.free = [p]
                o = (W if k else 0) + 128 * t
                e1 = act(to.qt[k].ap[:, :, o:o + 128], bank.ap[:, :].rearrange("p (a b) -> p a b", a=4), ACT.Copy,
                         p, ready, *to.qt[k].free)
                bank.free = [e1]
                return e1, act(to.qh[k].ap[:, :, o:o + 128], to.qt[k].ap[:, :, o:o + 128], ACT.Copy, e1, ready,
                               *to.qh[k].free)

            made = {}
            for n in range(NT + 1):
                if n < NT:
                    banks, sqs, sms, ss = project(n)
                    yield
                    p, v_done = v_chunk(c, to.v, n, x_of(n), w_of(2048 + 512 * half), 1.0 / WS, xs, c.w_in)
                    rn = inverse_norm(sms, ss)
                yield
                if n:
                    turn(0, n - 1, *made[n - 1][0])
                    yield
                if n < NT:
                    made[n] = rotate(n, banks, sqs, sms, rn)
                    yield
                if n:
                    qk32, qk16 = turn(1, n - 1, *made[n - 1][1])
                    yield
            for k in range(2):
                to.qt[k].free, to.qh[k].free = [], []
            to.v.free = []
            if half:
                x_split.free = [p]
            to.made = (qk32, qk16, v_done)

        def attend(u, before):
            c, (b, half), to = C[1], divmod(u, 2), C[u % 2]
            acc = C[b % 2].acc
            qk32, qk16, v_done = to.made
            next(before, None)
            yield
            m = c.sm.take()
            for tp in range(2):
                be, bo = c.ps.take(), c.ps.take()
                for bk in (be, bo):
                    mm(bk.ap[:, :], identb, maskp[tp], *bk.free, start=True, stop=False)
                for tq in range(2):
                    t = 2 * tp + tq
                    for i in range(4):
                        for g in range(4):
                            for e_, bk in enumerate((be, bo)):
                                rows = slice(64 * e_, 64 * e_ + 64)
                                o = 256 * tq + 64 * i
                                last = tq == 1 and i == 3 and g == 3
                                p = mm(bk.ap[32 * g:32 * g + 32, o:o + 64],
                                       to.qh[0].ap[rows, i, 128 * t + 32 * g:128 * t + 32 * g + 32],
                                       to.qh[1].ap[rows, i, 128 * t + 32 * g:128 * t + 32 * g + 64], qk16,
                                       start=False, stop=last, signal=last,
                                       tile_position=(64 * e_, 32 * g))
                for e_, bk in enumerate((be, bo)):
                    mx = reduce(m.ap[:, 16 * tp:16 * tp + 16].rearrange("p (t e i) -> p t e i", t=2, e=2)[:, :, e_, :],
                                bk.ap[:, :].rearrange("p (t i r) -> p t i r", t=2, i=4), ALU.max, p, *m.free)
                    bk.free = [mx]
                yield
                next(before, None)
            to.qh[0].free, to.qh[1].free = [p], [p]
            bank = c.ps.take()
            for t in range(NT):
                p = tr(bank.ap[0:8, 128 * t:128 * t + 128], m.ap[:, 8 * t:8 * t + 8], ident, mx, *bank.free,
                       signal=(t == NT - 1))
            m.free = [p]
            b3 = bank.ap[0:8, :].rearrange("p (t n) -> p t n", t=4)
            act(to.rhs.ap[96:104, :, 0:128], b3, ACT.Copy, p, *to.rhs.free, scale=-1.0)
            ng = act(to.rhs.ap[96:104, 0:3, 128:160], b3[:, 1:4, 0:32], ACT.Copy, scale=-1.0)
            bank.free = [ng]
            to.rhs.free = []
            yield
            next(before, None)

            def scores(t, pair):
                pt = c.pt.take() if pair == 0 else pts[t][0]
                banks = (c.ps.take(), c.ps.take())
                for e_, bk in enumerate(banks):
                    for y in range(2):
                        r = 4 * e_ + 2 * pair + y
                        mm(bk.ap[:, 160 * y:160 * y + 160], t_left[:, 128 * r:128 * r + 128],
                           to.rhs.ap[:, t, :], ng, ready, *bk.free, start=(y == 0), stop=False)
                for y in range(2):
                    for e_, bk in enumerate(banks):
                        rows = slice(64 * e_, 64 * e_ + 64)
                        i = 2 * pair + y
                        p = mm(bk.ap[:, 160 * y:160 * y + 160],
                               to.qt[1].ap[rows, i, W + 128 * t:W + 128 * t + 128],
                               to.qt[0].ap[rows, i, 128 * t:128 * t + 160], qk32,
                               start=False, stop=(y == 1), signal=(y == 1))
                ex = exp_split(c, banks, 320, pt, [160 * (4 * e_ + 2 * pair) for e_ in range(2)], p, AC,
                               DV if pair else GP)
                pts[t] = (pt, pts[t][1] + [ex] if pair else [ex])
                if t == NT - 1 and pair:
                    to.qt[0].free, to.qt[1].free, to.rhs.free = [p], [p], [p]

            def values(t):
                pt, ex = pts[t]
                banks = (c.ps.take(), c.ps.take())
                for e_, bk in enumerate(banks):
                    for i in range(4):
                        r = 4 * e_ + i
                        p = mm3(bk.ap[:, 65 * i:65 * i + 65],
                                tuple(pt.ap[:, z, 160 * r:160 * r + 128] for z in range(2)),
                                tuple(to.v.ap[:, z, t, 2 * i + e_, :] for z in range(2)), *ex, v_done, *bk.free,
                                start=(i == 0), stop=(i == 3), signal=(i == 3))
                if t:
                    prev = pts[t - 1][0]
                    for e_, bk in enumerate(banks):
                        for i in range(4):
                            r = 4 * e_ + i
                            p = mm3(bk.ap[0:32, 65 * i:65 * i + 65],
                                    tuple(prev.ap[96:128, z, 160 * r + 128:160 * r + 160] for z in range(2)),
                                    tuple(to.v.ap[96:128, z, t - 1, 2 * i + e_, :] for z in range(2)),
                                    start=False, stop=(i == 3), signal=(i == 3), tile_position=(96, 0))
                    prev_place = pts[t - 1][0]
                    prev_place.free = [p]
                if t == NT - 1:
                    pt.free = [p]
                    to.v.free = [p]
                wo_ = c.wu.take()
                for e_, bk in enumerate(banks):
                    rc = c.sm.take()
                    pv = bk.ap[:, 0:260].rearrange("p (a b) -> p a b", a=4)
                    d = recip(rc.ap[:, 0:4], pv[:, :, 64], p, *rc.free)
                    o = tt(DV, wo_.ap[:, :].rearrange("p (i e d) -> p i e d", i=4, e=2)[:, :, e_, :], pv[:, :, 0:64],
                           rc.ap[:, 0:4].unsqueeze(2).to_broadcast([128, 4, 64]), ALU.mult, d, *wo_.free)
                    rc.free = [o]
                    bk.free = [o]
                return wo_, o

            pts, outs, turned = {}, {}, {}

            def finish(t):
                turned[t] = finish_heads(c, C[t // 2].ot, outs[t][0], t, outs[t][1])

            def out(tp):
                return project_out(c, C[tp].ot, acc, half, tp, turned[2 * tp + 1], c.wo_in)

            for t in range(NT):
                scores(t, 0)
                yield
                next(before, None)
                if t >= 2:
                    finish(t - 2)
                    yield
                scores(t, 1)
                yield
                next(before, None)
                if t:
                    outs[t - 1] = values(t - 1)
                    yield

            def rest():
                outs[3] = values(3)
                yield
                out(0)
                yield
                finish(2)
                yield
                finish(3)
                yield
                done = out(1)
                if half == 0:
                    return
                yield
                a = tt(DV, xb[0:64, b, 0:S], xb[0:64, b, 0:S], acc.ap[0:64, :], ALU.add, done, x_ready[b], *x_read[b])
                a = tt(DV, xb[64:128, b, 1:S + 1], xb[64:128, b, 1:S + 1], acc.ap[64:128, :], ALU.add, done)
                acc.free = [a]
                x_ready[b] = a
                yield
                started = layernorm_start(c, xb[:, b, 0:S], a)
                yield
                started = layernorm_mid(c, started)
                yield
                wx = started[1]
                done, read = layernorm_end(c, started)
                xn_kept[b] = SP.dma(s_xo[b], xnd[b], wx.ap[:, :], done)
                wx.free = [xn_kept[b]]
                x_read[b] = [read]

            rests[u] = rest()

        def local_layer(middle):
            for _ in produce(0):
                pass
            before = iter(())
            for u in range(2 * NB):
                if u == NB:
                    middle()
                nxt = produce(u + 1) if u + 1 < 2 * NB else iter(())
                steps, made = 0, 0
                for _ in attend(u, before):
                    steps += 1
                    while made < steps * PSTEPS * AHEAD / CSTEPS:
                        made += 1
                        next(nxt, None)
                for _ in before:
                    pass
                for _ in nxt:
                    pass
                before = rests[u]
            for _ in before:
                pass

        def feed(c, b, li):
            us = []
            xin, t_in = xn_in.pop(b)
            for j in range(3):
                n = FP[j]
                ba, bg = c.ps.take(), c.ps.take()
                mm(ba.ap[0:n, :], w1r[:, 128 * j:128 * j + n], xin.ap, t_in, c.w1_in, *ba.free)
                p = mm(bg.ap[0:n, :], w1r[:, FF + 128 * j:FF + 128 * j + n], xin.ap, *bg.free, signal=True)
                g, u = c.wk.take(), c.wu.take()
                ge = act(g.ap[0:n, :], bg.ap[0:n, :], ACT.Gelu, p, c.b1_in, *g.free, bias=b1s[0:n, 3 + j:4 + j])
                ud = stt(u.ap[0:n, :], ba.ap[0:n, :], b1s[0:n, j:j + 1], g.ap[0:n, :], ALU.add, ALU.mult, ge, *u.free)
                bg.free, ba.free, g.free = [ge], [ud], [ud]
                us.append((u, ud))
                yield
            xin.free = [p]
            if b + 4 < NB:
                fetch(xin, b + 4)
            bank = c.ps.take()
            for j in range(3):
                n = FP[j]
                p = mm(bank.ap[:, :], w2r[0:n, j, :], us[j][0].ap[0:n, :], us[j][1], c.w2_in, *bank.free,
                       start=(j == 0), stop=(j == 2), signal=(j == 2))
                us[j][0].free = [p]
            us[0][0].free = us[1][0].free = us[2][0].free = [p]
            w2_read.append(p)
            b2 = t_vec[:, V_LAYER + 10 * li + 2:V_LAYER + 10 * li + 3]
            a = stt(xb[0:64, b, 0:S], bank.ap[0:64, :], b2[0:64, :], xb[0:64, b, 0:S], ALU.add, ALU.add, p,
                    x_ready[b], *x_read[b])
            a = stt(xb[64:128, b, 1:S + 1], bank.ap[64:128, :], b2[64:128, :], xb[64:128, b, 1:S + 1],
                    ALU.add, ALU.add, p)
            bank.free = [a]
            x_ready[b] = a
            x_read[b] = []
            yield

        def together(works, offset):
            live = [[(n * offset), n, (y for w in ws for y in w)] for n, ws in enumerate(works)]
            while live:
                live.sort(key=lambda x: (x[0], x[1]))
                before = work[0]
                try:
                    weight = next(live[0][2]) or 1.0
                    live[0][0] += max(work[0] - before, 64) * weight
                except StopIteration:
                    live.pop(0)

        def fetch(place, b):
            xn_in[b] = (place, SP.dma(s_xi[b], place.ap, xnd[b], xn_kept[b], *place.free))

        s_x1 = [slot(f"x1_{b}") for b in range(NB)]
        x1d = nc.dram_tensor("x1_keep", [NB, 128, S], F32).ap()
        kept = {}
        xnd = nc.dram_tensor("xn_keep", [NB, 128, S], F32).ap()
        s_xo = [slot(f"xo{b}") for b in range(NB)]
        s_xi = [slot(f"xi{b}") for b in range(NB)]
        xn_kept, xn_in, rests = {}, {}, {}
        for n, c in enumerate(C):
            c.n = n
            c.obig = Place(c.qt[1].ap.rearrange("p a b -> p (a b)")[:, 544:1568].rearrange("p (a d) -> p a d", a=4))
        both = Ring([p for c in C for p in c.pt.places])
        together([[causal(C[n], b) for b in range(n, NB, 2)] for n in range(2)], 24000)
        for c in C:
            c.pt = both
        fold_read = [(PE.name, PE.count, PE.sem)]

        s_w1, s_w2, s_scl, s_tab, s_st = slot("w1"), slot("w2"), slot("scl"), slot("tab"), [slot("st0"), slot("st1")]
        w2_read = []
        state = {"rot": None, "b1d": None}

        def load_tables(li, free):
            scl_in = SP.dma(s_scl, t_scl[:, :, :].rearrange("p a b -> p (a b)"), scl[li], state["rot"])
            for n in range(2):
                tab_in = SP.dma(s_tab, t_rots[:, n, :], tab[n], *free)
            rot = tt(GP, t_rot[0], t_rot[0], t_scl[:, :, :].unsqueeze(1).to_broadcast([128, NT, 2, DH]), ALU.mult,
                     scl_in, tab_in)
            for e_ in range(2):
                half_ = t_rot[1][:, :, :, 32 * e_:32 * e_ + 32]
                rot = tt(GP, half_, half_,
                         t_scl[:, :, 32 * (1 - e_):32 * (1 - e_) + 32].unsqueeze(1).to_broadcast([128, NT, 2, 32]),
                         ALU.mult, rot)
            state["rot"] = rot

        def load_qkv(li, free):
            for n in range(6):
                st = wstage.take()
                t_st = SP.dma(s_st[n % 2], st.ap[:, :], wqkv[li, :, 512 * n:512 * n + 512], *st.free)
                hi = wsplit[:, 512 * n:512 * n + 512]
                a = act(hi, st.ap[:, :], ACT.Copy, t_st, *free, scale=WS)
                state["w_in"] = stt(wsplit[:, 3072 + 512 * n:3584 + 512 * n], st.ap[:, :], WS, hi, ALU.mult,
                                    ALU.subtract, a)
                st.free = [state["w_in"]]
                yield 180.0

        def load_out(li, free):
            state["wo_in"] = SP.dma(s_wo, wout[:, :, :], wof[li].rearrange("(a p) c -> p a c", p=128), *free)

        load_tables(0, fold_read)
        for _ in load_qkv(0, fold_read):
            pass
        load_out(0, fold_read)
        for li in range(L):
            w1_in = SP.dma(s_w1, w1r, w1[li], *w2_read, state["b1d"], *(fold_read if li == 0 else []))
            for j in range(3):
                w2_in = SP.dma(s_w2, w2r[0:FP[j], j, :], w2[li, 128 * j:128 * j + FP[j], :], *w2_read)
            w1_free = list(w2_read)
            for c in C:
                c.w_in, c.wo_in, c.rot, c.w2_in = state["w_in"], state["wo_in"], state["rot"], w2_in

            def scale_w1():
                bank = C[0].ps.take()
                vl = V_LAYER + 10 * li
                for k in range(2):
                    for j in range(3):
                        n = FP[j]
                        pb = mm(bank.ap[0:n, 3 * k + j:3 * k + j + 1], w1r[:, FF * k + 128 * j:FF * k + 128 * j + n],
                                t_vec[:, vl + 1:vl + 2], w1_in, *bank.free, start=(k == 0 and j == 0), stop=True,
                                signal=True)
                for k in range(2):
                    tt(DV, b1s[:, 3 * k:3 * k + 2], bank.ap[:, 3 * k:3 * k + 2],
                       t_vec[:, vl + 4 + 3 * k:vl + 6 + 3 * k], ALU.add, pb, *w1_free)
                    b1d = tt(DV, b1s[0:FP[2], 3 * k + 2:3 * k + 3], bank.ap[0:FP[2], 3 * k + 2:3 * k + 3],
                             t_vec[0:FP[2], vl + 6 + 3 * k:vl + 7 + 3 * k], ALU.add)
                bank.free = [b1d]
                w1s = ts(DV, w1r, w1r, t_vec[:, vl:vl + 1], None, ALU.mult, None, b1d)
                for c in C:
                    c.w1_in, c.b1_in = w1s, b1d

            tables("natural_log_exp_and_others")
            local_layer(scale_w1)
            tables("gelu_and_others")
            layer_read = [(PE.name, PE.count, PE.sem), (GP.name, GP.count, GP.sem), (DV.name, DV.count, DV.sem)]
            w2_read.clear()
            for c in C:
                fetch(Place(c.acc.ap[:, :]), c.n)
                fetch(Place(c.xs.ap[:, :, :].rearrange("p a b -> p (a b)").bitcast(F32)), c.n + 2)
            works = [[feed(C[n], b, li) for b in range(n, NB, 2)] for n in range(2)]
            if li + 1 < L:
                load_out(li + 1, layer_read)
                load_tables(li + 1, layer_read)
                works.append([load_qkv(li + 1, layer_read)])
            together(works, 0)
            for c in C:
                c.acc.free, c.xs.free = [w2_read[-1]], [w2_read[-1]]
            state["b1d"] = w2_read[-1]

        s_out, s_x1r = slot("out"), [slot(f"x1r{b}") for b in range(NB)]
        fold_done = layer_read
        for b in range(NB):
            y = C[b % 2].qt[b // 4].ap[:, b // 2 % 2, 0:S]
            back = SP.dma(s_x1r[b], y, x1d[b], kept[b], *fold_done)
            z = stt(y[0:64, :], xb[0:64, b, 0:S], t_mod[0:64, 5, b:b + 1], y[0:64, :], ALU.mult, ALU.add,
                    back, x_ready[b])
            z = stt(y[64:128, :], xb[64:128, b, 1:S + 1], t_mod[64:128, 5, b:b + 1], y[64:128, :],
                    ALU.mult, ALU.add)
            o = SP.dma(s_out, out[b], y, z)
        SP.wait(o)

        block = ctx.enter_context(nc.Block())

        @block.sync
        def _(e):
            SP.play(e)

        @block.tensor
        def _(e):
            PE.play(e)

        @block.scalar
        def _(e):
            AC.play(e)

        @block.vector
        def _(e):
            DV.play(e)

        @block.gpsimd
        def _(e):
            GP.play(e)


def kernel(**inputs):
    import concourse.bacc as _bacc
    from concourse.bass_utils import run_bass_kernel_spmd as _run

    a = {k: np.asarray(v) for k, v in inputs.items()}
    f = np.float32
    vecs = np.zeros((128, V_COLS), f)
    vecs[:, V_BO] = a["L0_attn_bo"]
    for li in range(L):
        o = V_LAYER + 10 * li
        vecs[:, o] = a["L0_ffn_ln_g"][li]
        vecs[:, o + 1] = a["L0_ffn_ln_b"][li]
        vecs[:, o + 2] = a["L0_ffn_b2"][li]
        for k in range(2):
            for j in range(3):
                vecs[0:FP[j], o + 4 + 3 * k + j] = a["L0_ffn_b1"][li][FF * k + 128 * j:FF * k + 128 * j + FP[j]]
    scl = np.concatenate([a["L0_ffn_q_scale"], a["L0_ffn_k_scale"]], 1)
    arrays = {
        "xt": a["L0_attn_x"].transpose(0, 2, 1),
        "wqt": a["L0_attn_Wq"].T, "wkt": a["L0_attn_Wk"].T, "wv": a["L0_attn_Wv"], "wo": a["L0_attn_Wo"],
        "wqkv": a["L0_ffn_Wqkv"], "wof": a["L0_ffn_Wo"], "w1": a["L0_ffn_W1"], "w2": a["L0_ffn_W2"],
        "vecs": vecs, "scl": np.broadcast_to(scl[:, None, :], (L, 128, 2 * DH)), "ct": a["L0_c"].T, "wmod": a["L0_wmod"],
    }
    arrays.update(constants())
    arrays = {k: np.ascontiguousarray(v) for k, v in arrays.items()}
    nc = _bacc.Bacc("TRN2", target_bir_lowering=False, num_devices=1)
    args = {k: nc.dram_tensor(k, v.shape, mybir.dt.from_np(v.dtype), kind="ExternalInput").ap() for k, v in arrays.items()}
    args["out"] = nc.dram_tensor("out", (NB, 128, S), F32, kind="ExternalOutput").ap()
    program(nc, **args)
    r = _run(nc, [arrays], core_ids=[0])
    return r.results[0]["out"].transpose(0, 2, 1)
```
